# Optimizing a Trainium2 kernel written in Bass

```python
import numpy as np
import jax
import jax.numpy as jnp

def _softmax(x, axis=-1):
    return jax.nn.softmax(x, axis=axis)

def _gelu(x):
    return jax.nn.gelu(x, approximate=True)

def _silu(x):
    return jax.nn.silu(x)

def _sigmoid(x):
    return jax.nn.sigmoid(x)

def _layernorm(x, axis=-1, eps=1e-05):
    m = jnp.mean(x, axis=axis, keepdims=True)
    v = jnp.var(x, axis=axis, keepdims=True)
    return (x - m) / jnp.sqrt(v + eps)

def _scatter_add(tgt, idx, src, axis=0):
    return tgt.at[idx].add(src)

def _segment_sum(src, seg, n):
    return jax.ops.segment_sum(src, seg, n)
kernel_name = 'mk_dlrm_tower_d1_rec_r8_261d0f'

def setup_inputs(seed: int=0):
    np.random.seed(seed)
    _w = jnp.asarray

    def _rec_inputs():
        import jax
        import jax.numpy as jnp
        _tk = jax.random.key(seed)
        dense_ctx = jax.random.normal(jax.random.fold_in(_tk, 190), (512, 16), jnp.float32)
        ids = jnp.stack([jax.random.randint(jax.random.fold_in(_tk, 200 + f), (512,), 0, v, jnp.int32) for f, v in enumerate([125000, 1250, 125000, 1250, 125000, 1250, 1000, 125000, 1250, 1000, 1000, 1000, 12500, 1250, 1000, 1000, 1250, 1000, 125000, 1250, 1250, 125000, 125000, 125000, 1000, 1250, 12500, 125000, 1250, 1250, 12500, 125000, 1000, 1250, 1000, 1000, 125000, 125000, 1250, 125000])], axis=1)
        tbl_0 = 0.05 * jax.random.normal(jax.random.fold_in(_tk, 500 + 0), (125000, 16), jnp.float32)
        tbl_1 = 0.05 * jax.random.normal(jax.random.fold_in(_tk, 500 + 1), (1250, 16), jnp.float32)
        tbl_2 = 0.05 * jax.random.normal(jax.random.fold_in(_tk, 500 + 2), (125000, 16), jnp.float32)
        tbl_3 = 0.05 * jax.random.normal(jax.random.fold_in(_tk, 500 + 3), (1250, 16), jnp.float32)
        tbl_4 = 0.05 * jax.random.normal(jax.random.fold_in(_tk, 500 + 4), (125000, 16), jnp.float32)
        tbl_5 = 0.05 * jax.random.normal(jax.random.fold_in(_tk, 500 + 5), (1250, 16), jnp.float32)
        tbl_6 = 0.05 * jax.random.normal(jax.random.fold_in(_tk, 500 + 6), (1000, 16), jnp.float32)
        tbl_7 = 0.05 * jax.random.normal(jax.random.fold_in(_tk, 500 + 7), (125000, 16), jnp.float32)
        tbl_8 = 0.05 * jax.random.normal(jax.random.fold_in(_tk, 500 + 8), (1250, 16), jnp.float32)
        tbl_9 = 0.05 * jax.random.normal(jax.random.fold_in(_tk, 500 + 9), (1000, 16), jnp.float32)
        tbl_10 = 0.05 * jax.random.normal(jax.random.fold_in(_tk, 500 + 10), (1000, 16), jnp.float32)
        tbl_11 = 0.05 * jax.random.normal(jax.random.fold_in(_tk, 500 + 11), (1000, 16), jnp.float32)
        tbl_12 = 0.05 * jax.random.normal(jax.random.fold_in(_tk, 500 + 12), (12500, 16), jnp.float32)
        tbl_13 = 0.05 * jax.random.normal(jax.random.fold_in(_tk, 500 + 13), (1250, 16), jnp.float32)
        tbl_14 = 0.05 * jax.random.normal(jax.random.fold_in(_tk, 500 + 14), (1000, 16), jnp.float32)
        tbl_15 = 0.05 * jax.random.normal(jax.random.fold_in(_tk, 500 + 15), (1000, 16), jnp.float32)
        tbl_16 = 0.05 * jax.random.normal(jax.random.fold_in(_tk, 500 + 16), (1250, 16), jnp.float32)
        tbl_17 = 0.05 * jax.random.normal(jax.random.fold_in(_tk, 500 + 17), (1000, 16), jnp.float32)
        tbl_18 = 0.05 * jax.random.normal(jax.random.fold_in(_tk, 500 + 18), (125000, 16), jnp.float32)
        tbl_19 = 0.05 * jax.random.normal(jax.random.fold_in(_tk, 500 + 19), (1250, 16), jnp.float32)
        tbl_20 = 0.05 * jax.random.normal(jax.random.fold_in(_tk, 500 + 20), (1250, 16), jnp.float32)
        tbl_21 = 0.05 * jax.random.normal(jax.random.fold_in(_tk, 500 + 21), (125000, 16), jnp.float32)
        tbl_22 = 0.05 * jax.random.normal(jax.random.fold_in(_tk, 500 + 22), (125000, 16), jnp.float32)
        tbl_23 = 0.05 * jax.random.normal(jax.random.fold_in(_tk, 500 + 23), (125000, 16), jnp.float32)
        tbl_24 = 0.05 * jax.random.normal(jax.random.fold_in(_tk, 500 + 24), (1000, 16), jnp.float32)
        tbl_25 = 0.05 * jax.random.normal(jax.random.fold_in(_tk, 500 + 25), (1250, 16), jnp.float32)
        tbl_26 = 0.05 * jax.random.normal(jax.random.fold_in(_tk, 500 + 26), (12500, 16), jnp.float32)
        tbl_27 = 0.05 * jax.random.normal(jax.random.fold_in(_tk, 500 + 27), (125000, 16), jnp.float32)
        tbl_28 = 0.05 * jax.random.normal(jax.random.fold_in(_tk, 500 + 28), (1250, 16), jnp.float32)
        tbl_29 = 0.05 * jax.random.normal(jax.random.fold_in(_tk, 500 + 29), (1250, 16), jnp.float32)
        tbl_30 = 0.05 * jax.random.normal(jax.random.fold_in(_tk, 500 + 30), (12500, 16), jnp.float32)
        tbl_31 = 0.05 * jax.random.normal(jax.random.fold_in(_tk, 500 + 31), (125000, 16), jnp.float32)
        tbl_32 = 0.05 * jax.random.normal(jax.random.fold_in(_tk, 500 + 32), (1000, 16), jnp.float32)
        tbl_33 = 0.05 * jax.random.normal(jax.random.fold_in(_tk, 500 + 33), (1250, 16), jnp.float32)
        tbl_34 = 0.05 * jax.random.normal(jax.random.fold_in(_tk, 500 + 34), (1000, 16), jnp.float32)
        tbl_35 = 0.05 * jax.random.normal(jax.random.fold_in(_tk, 500 + 35), (1000, 16), jnp.float32)
        tbl_36 = 0.05 * jax.random.normal(jax.random.fold_in(_tk, 500 + 36), (125000, 16), jnp.float32)
        tbl_37 = 0.05 * jax.random.normal(jax.random.fold_in(_tk, 500 + 37), (125000, 16), jnp.float32)
        tbl_38 = 0.05 * jax.random.normal(jax.random.fold_in(_tk, 500 + 38), (1250, 16), jnp.float32)
        tbl_39 = 0.05 * jax.random.normal(jax.random.fold_in(_tk, 500 + 39), (125000, 16), jnp.float32)
        _rk = jax.random.fold_in(_tk, 7)
        W_top1 = 0.05 * jax.random.normal(jax.random.fold_in(_tk, 801), (400, 512), jnp.float32)
        W_top2 = 0.0441942 * jax.random.normal(jax.random.fold_in(_tk, 802), (512, 256), jnp.float32)
        W_top3 = 0.0625 * jax.random.normal(jax.random.fold_in(_tk, 803), (256, 1), jnp.float32)
        b_top1 = jnp.zeros((512,), jnp.float32)
        b_top2 = jnp.zeros((256,), jnp.float32)
        return (dense_ctx, ids, tbl_0, tbl_1, tbl_2, tbl_3, tbl_4, tbl_5, tbl_6, tbl_7, tbl_8, tbl_9, tbl_10, tbl_11, tbl_12, tbl_13, tbl_14, tbl_15, tbl_16, tbl_17, tbl_18, tbl_19, tbl_20, tbl_21, tbl_22, tbl_23, tbl_24, tbl_25, tbl_26, tbl_27, tbl_28, tbl_29, tbl_30, tbl_31, tbl_32, tbl_33, tbl_34, tbl_35, tbl_36, tbl_37, tbl_38, tbl_39, W_top1, b_top1, W_top2, b_top2, W_top3)
    dense_ctx, ids, tbl_0, tbl_1, tbl_2, tbl_3, tbl_4, tbl_5, tbl_6, tbl_7, tbl_8, tbl_9, tbl_10, tbl_11, tbl_12, tbl_13, tbl_14, tbl_15, tbl_16, tbl_17, tbl_18, tbl_19, tbl_20, tbl_21, tbl_22, tbl_23, tbl_24, tbl_25, tbl_26, tbl_27, tbl_28, tbl_29, tbl_30, tbl_31, tbl_32, tbl_33, tbl_34, tbl_35, tbl_36, tbl_37, tbl_38, tbl_39, W_top1, b_top1, W_top2, b_top2, W_top3 = _rec_inputs()

    def _L0_rec_setup():
        import jax, jax.numpy as jnp
        import numpy as np
        B, M, D = (512, 40, 16)
        DIMS = [128, 128, 128]
        key = jax.random.key(seed)
        k_x, k0, k1, k2 = jax.random.split(key, 4)
        scale = lambda fan_in: (2.0 / fan_in) ** 0.5
        x0 = jax.random.normal(k_x, (B, M, D), dtype=jnp.float32)
        kern0 = jax.random.normal(k0, (DIMS[0], M, M), dtype=jnp.float32) * scale(M * M)
        kern1 = jax.random.normal(k1, (DIMS[1], DIMS[0], M), dtype=jnp.float32) * scale(DIMS[0] * M)
        kern2 = jax.random.normal(k2, (DIMS[2], DIMS[1], M), dtype=jnp.float32) * scale(DIMS[1] * M)
        return {'x0': x0, 'k0': kern0, 'k1': kern1, 'k2': kern2}
    _L0_rec_all = _L0_rec_setup()
    _L0_rec_in = {k: v for k, v in _L0_rec_all.items() if k in ('k0', 'k1', 'k2')}
    del _L0_rec_all
    return {'dense_ctx': dense_ctx, 'ids': ids, 'tbl_0': tbl_0, 'tbl_1': tbl_1, 'tbl_2': tbl_2, 'tbl_3': tbl_3, 'tbl_4': tbl_4, 'tbl_5': tbl_5, 'tbl_6': tbl_6, 'tbl_7': tbl_7, 'tbl_8': tbl_8, 'tbl_9': tbl_9, 'tbl_10': tbl_10, 'tbl_11': tbl_11, 'tbl_12': tbl_12, 'tbl_13': tbl_13, 'tbl_14': tbl_14, 'tbl_15': tbl_15, 'tbl_16': tbl_16, 'tbl_17': tbl_17, 'tbl_18': tbl_18, 'tbl_19': tbl_19, 'tbl_20': tbl_20, 'tbl_21': tbl_21, 'tbl_22': tbl_22, 'tbl_23': tbl_23, 'tbl_24': tbl_24, 'tbl_25': tbl_25, 'tbl_26': tbl_26, 'tbl_27': tbl_27, 'tbl_28': tbl_28, 'tbl_29': tbl_29, 'tbl_30': tbl_30, 'tbl_31': tbl_31, 'tbl_32': tbl_32, 'tbl_33': tbl_33, 'tbl_34': tbl_34, 'tbl_35': tbl_35, 'tbl_36': tbl_36, 'tbl_37': tbl_37, 'tbl_38': tbl_38, 'tbl_39': tbl_39, 'W_top1': W_top1, 'b_top1': b_top1, 'W_top2': W_top2, 'b_top2': b_top2, 'W_top3': W_top3, 'L0_rec_k0': _L0_rec_in['k0'], 'L0_rec_k1': _L0_rec_in['k1'], 'L0_rec_k2': _L0_rec_in['k2']}

def reference(dense_ctx, ids, tbl_0, tbl_1, tbl_2, tbl_3, tbl_4, tbl_5, tbl_6, tbl_7, tbl_8, tbl_9, tbl_10, tbl_11, tbl_12, tbl_13, tbl_14, tbl_15, tbl_16, tbl_17, tbl_18, tbl_19, tbl_20, tbl_21, tbl_22, tbl_23, tbl_24, tbl_25, tbl_26, tbl_27, tbl_28, tbl_29, tbl_30, tbl_31, tbl_32, tbl_33, tbl_34, tbl_35, tbl_36, tbl_37, tbl_38, tbl_39, W_top1, b_top1, W_top2, b_top2, W_top3, L0_rec_k0, L0_rec_k1, L0_rec_k2):
    import jax
    import jax.numpy as jnp

    def _L0_rec_ref(x0, k0, k1, k2):
        import jax, jax.numpy as jnp
        import numpy as np
        B, M, D = (512, 40, 16)
        DIMS = [128, 128, 128]
        x = x0
        outputs = []
        for k in (k0, k1, k2):
            x = jnp.einsum('bhd,bmd,ohm->bod', x, x0, k)
            outputs.append(jnp.sum(x, axis=-1))
        return jnp.concatenate(outputs, axis=1)
    e = jnp.stack([tbl_0[ids[:, 0]], tbl_1[ids[:, 1]], tbl_2[ids[:, 2]], tbl_3[ids[:, 3]], tbl_4[ids[:, 4]], tbl_5[ids[:, 5]], tbl_6[ids[:, 6]], tbl_7[ids[:, 7]], tbl_8[ids[:, 8]], tbl_9[ids[:, 9]], tbl_10[ids[:, 10]], tbl_11[ids[:, 11]], tbl_12[ids[:, 12]], tbl_13[ids[:, 13]], tbl_14[ids[:, 14]], tbl_15[ids[:, 15]], tbl_16[ids[:, 16]], tbl_17[ids[:, 17]], tbl_18[ids[:, 18]], tbl_19[ids[:, 19]], tbl_20[ids[:, 20]], tbl_21[ids[:, 21]], tbl_22[ids[:, 22]], tbl_23[ids[:, 23]], tbl_24[ids[:, 24]], tbl_25[ids[:, 25]], tbl_26[ids[:, 26]], tbl_27[ids[:, 27]], tbl_28[ids[:, 28]], tbl_29[ids[:, 29]], tbl_30[ids[:, 30]], tbl_31[ids[:, 31]], tbl_32[ids[:, 32]], tbl_33[ids[:, 33]], tbl_34[ids[:, 34]], tbl_35[ids[:, 35]], tbl_36[ids[:, 36]], tbl_37[ids[:, 37]], tbl_38[ids[:, 38]], tbl_39[ids[:, 39]]], axis=1)
    z = _L0_rec_ref(e, L0_rec_k0, L0_rec_k1, L0_rec_k2)
    z = z.reshape(z.shape[0], -1)
    h = jnp.concatenate([z, dense_ctx], axis=1)
    h = jnp.maximum(h @ W_top1 + b_top1, 0.0)
    h = jnp.maximum(h @ W_top2 + b_top2, 0.0)
    y = h @ W_top3
    return y

_drawn_inputs = setup_inputs


def setup_inputs(seed=0):
    import zlib

    import numpy as np

    out = dict(_drawn_inputs(seed))
    spreads = {'b_top1': (0.0, 0.528), 'b_top2': (0.0, 0.1)}
    factors = {'tbl_0': 7.591,
     'tbl_1': 6.686,
     'tbl_2': 6.364,
     'tbl_3': 6.631,
     'tbl_4': 6.862,
     'tbl_5': 7.075,
     'tbl_6': 7.29,
     'tbl_7': 7.436,
     'tbl_8': 6.744,
     'tbl_9': 7.481,
     'tbl_10': 7.136,
     'tbl_11': 6.693,
     'tbl_12': 6.404,
     'tbl_13': 6.931,
     'tbl_14': 6.94,
     'tbl_15': 7.043,
     'tbl_16': 6.983,
     'tbl_17': 6.378,
     'tbl_18': 7.213,
     'tbl_19': 6.766,
     'tbl_20': 7.567,
     'tbl_21': 7.93,
     'tbl_22': 7.634,
     'tbl_23': 6.729,
     'tbl_24': 7.581,
     'tbl_25': 6.688,
     'tbl_26': 6.925,
     'tbl_27': 6.852,
     'tbl_28': 6.322,
     'tbl_29': 7.125,
     'tbl_30': 7.16,
     'tbl_31': 6.972,
     'tbl_32': 6.914,
     'tbl_33': 6.189,
     'tbl_34': 7.025,
     'tbl_35': 6.541,
     'tbl_36': 6.805,
     'tbl_37': 6.144,
     'tbl_38': 6.807,
     'tbl_39': 6.667,
     'L0_rec_k1': 8.0,
     'L0_rec_k2': 8.0}
    for name, (base, spread) in spreads.items():
        noise = np.random.default_rng([zlib.crc32(name.encode()), seed]).standard_normal(out[name].shape)
        drawn = base * np.exp(spread * noise) if base else spread * noise
        out[name] = jnp.asarray(drawn.astype(out[name].dtype))
    for name, factor in factors.items():
        out[name] = (out[name] * factor).astype(out[name].dtype)
    return out
```

```python
from contextlib import ExitStack

import concourse.bass as bass
from concourse import mybir

F32 = mybir.dt.float32
F32R = mybir.dt.float32r
BF16 = mybir.dt.bfloat16
I32 = mybir.dt.int32
ALU = mybir.AluOpType
ACT = mybir.ActivationFunctionType
AX = mybir.AxisListType

B = 512
M = 40
D = 16
H = 128
DENSE = 16
N1, N2 = 512, 256

P = 128
TILES = B // P
CH = 512
CHUNKS = D * P // CH
DQ = D // 4
PARTS = 3
XK = PARTS * M

SHIFTS = M // 2 + 1
S_IN = P // M
K1B = SHIFTS // S_IN
PAIRS = (K1B + 1) // 2

R = 4
HG = H // 32
MJ = M // R
UNITS = MJ
HALVES = 2 * UNITS * CHUNKS
RING = 4
LAG = 5
RAW_LAG = 2
VB = 4

LOW = (("P", "P", "P", "D"), ("P", "P", "D", "R"))

GB = 8
GROUPS = P // GB


def pool_cols(v):
    return LOW[v // 2 % 2][2 * (v % 2):2 * (v % 2) + 2].count("P")


def pool_ops(v):
    return sum(pool_cols(x) > 0 for x in range(v + 1))


def block_kind(v, i):
    return LOW[v // 2 % 2][2 * (v % 2) + i]


def dve_ops(v):
    return sum(block_kind(x, i) == "D" for x in range(v + 1) for i in range(2))


def has_raw(v):
    return any(block_kind(v, i) == "R" for i in range(2))


def raw_ops(v):
    return sum(has_raw(x) for x in range(v + 1))


RAWJ = [j for j in range(MJ) if "R" in LOW[j % 2]]
RAWG = LOW[1].index("R")


def build(nc, t_):
    ctx = ExitStack()
    with ctx:
        def sb(name, shape, dt=F32):
            return ctx.enter_context(nc.sbuf_tensor(name, shape, dt))

        def sem(name):
            return ctx.enter_context(nc.semaphore(name))

        ids_now = sb("ids_now", [P, M], I32)
        emb = sb("emb", [P, M * D])
        rest = sb("rest", [P, D, M])
        parts = sb("parts", [P, D, XK], BF16)
        x0s = sb("x0s", [XK, CHUNKS * CH], BF16)
        xh = sb("xh", [P, CHUNKS * CH])
        u = sb("u", [P, CHUNKS, HG, CH])
        u_flat = u[:, :, :, :].rearrange("p q g n -> p (q g n)")
        prod = sb("prod", [P, RING, 2 * CH])
        prod_hi = sb("prod_hi", [P, RING, 2 * CH], F32R)
        prod_lo = sb("prod_lo", [P, RING, 2 * CH], F32R)
        k1h = sb("k1h", [P, MJ, HG, H], F32R)
        k1l = sb("k1l", [P, MJ, HG, H], F32R)
        k1raw = sb("k1raw", [P, len(RAWJ), H])
        k2w = sb("k2w", [P, M, H])
        k0w = sb("k0w", [S_IN * M, K1B, H])
        sel = sb("sel", [XK, MJ * P], BF16)
        rot = sb("rot", [XK, (K1B + 1) * S_IN * M], BF16)
        pick = sb("pick", [XK, M], BF16)
        ident = sb("ident", [P, P])
        ident_b = sb("ident_b", [P, P], BF16)
        mask = sb("mask", [P, GB])
        diag = sb("diag", [P, 2, GB, M])
        x2t = sb("x2t", [P, 2, P])
        z = [sb(f"z{i}", [P, B]) for i in range(3)]
        dense = sb("dense", [DENSE, B])
        w1 = sb("w1", [P, 3, N1])
        w1d = sb("w1d", [DENSE, N1])
        w2 = sb("w2", [P, N1 // P, N2])
        w3 = sb("w3", [P, N2 // P])
        b1 = sb("b1", [P, N1 // P])
        b2 = sb("b2", [P, N2 // P])
        y = sb("y", [1, B])

        k1_raw_all = u_flat[:, 0:MJ * HG * H]
        k0_turned = u_flat[0:S_IN * M, MJ * HG * H:MJ * HG * H + K1B * H]
        consts = prod[:, :, :].rearrange("p r n -> p (r n)")
        u1 = prod[0:S_IN * M, 2:4, :].rearrange("p r n -> p (r n)")
        gsb = u_flat[:, 0:M * P].rearrange("p (m b) -> p m b", m=M)
        mlp = prod[:, :, :].rearrange("p r n -> p (r n)")
        h1 = mlp[:, 0:4 * B].rearrange("p (k b) -> p k b", k=4)
        h2 = mlp[:, 4 * B:6 * B].rearrange("p (k b) -> p k b", k=2)
        SEL_N, ROT_N = MJ * P, (K1B + 1) * S_IN * M

        ps = ctx.enter_context(nc.psum_tensor("ps", [P, 8, CH], F32))
        ACC, VBANK, XBANK = 0, 2, 6
        ps_b = [ps[0:XK, XBANK + i, :].bitcast(BF16) for i in range(2)]

        s_ids = sem("s_ids")
        s_const = sem("s_const")
        s_k1 = sem("s_k1")
        s_k0 = sem("s_k0")
        s_tail = sem("s_tail")
        s_gather = sem("s_gather")
        s_copies = [sem(f"s_copies{q}") for q in range(CHUNKS)]
        s_out = sem("s_out")
        s_sel = sem("s_sel")
        s_k1h = sem("s_k1h")
        s_k1l = sem("s_k1l")
        s_k0w = sem("s_k0w")
        s_part0 = sem("s_part0")
        s_rest = sem("s_rest")
        s_part1 = sem("s_part1")
        s_parts = sem("s_parts")
        s_turned = sem("s_turned")
        s_x0s = sem("s_x0s")
        s_u1_ps = sem("s_u1_ps")
        s_u1 = sem("s_u1")
        s_v1 = sem("s_v1")
        s_p1 = sem("s_p1")
        s_mm1 = sem("s_mm1")
        s_x1 = sem("s_x1")
        s_z1 = sem("s_z1")
        s_v2 = sem("s_v2")
        s_p2 = sem("s_p2")
        s_hi = sem("s_hi")
        s_lo_pool = sem("s_lo_pool")
        s_lo_dve = sem("s_lo_dve")
        s_raw = sem("s_raw")
        s_mm2 = sem("s_mm2")
        s_x2 = sem("s_x2")
        s_z2 = sem("s_z2")
        s_x2t_ps = sem("s_x2t_ps")
        s_x2t = sem("s_x2t")
        s_x0t_ps = sem("s_x0t_ps")
        s_diag = sem("s_diag")
        s_g_ps = sem("s_g_ps")
        s_g = sem("s_g")
        s_z3_ps = sem("s_z3_ps")
        s_z3 = sem("s_z3")
        s_h1_ps = sem("s_h1_ps")
        s_h1 = sem("s_h1")
        s_h2_ps = sem("s_h2_ps")
        s_h2 = sem("s_h2")
        s_y_ps = sem("s_y_ps")
        s_y = sem("s_y")
        passed = sem("passed")

        def wait_alone(eng, s, value):
            eng.wait_ge(s, value)
            eng.sem_inc(passed, 1)

        block = ctx.enter_context(nc.Block())

        @block.sync
        def _(sp):
            ids_h = t_["ids"]
            sp.dma_start(ids_now[:, :], ids_h[0:P, :]).then_inc(s_ids, 16)
            sp.dma_start(consts[0:XK, 0:SEL_N + ROT_N + M], t_["consts"]).then_inc(s_const, 16)
            sp.dma_start(ident[:, :], t_["ident"]).then_inc(s_const, 16)
            sp.dma_start(k0w[:, :, :], t_["k0_straight"]).then_inc(s_k0, 16)
            sp.dma_start(k0_turned, t_["k0_turned"]).then_inc(s_k0, 16)
            sp.dma_start(k1_raw_all, t_["k1"]).then_inc(s_k1, 16)
            sp.dma_start(k1raw[:, :, :],
                         t_["k1"].rearrange("p (j g o) -> p j g o", j=MJ, g=HG)[:, RAWJ[0]::2, RAWG, :]
                         ).then_inc(s_tail, 16)
            sp.dma_start(mask[:, :], t_["mask"]).then_inc(s_tail, 16)
            sp.dma_start(k2w[:, :, :], t_["k2"]).then_inc(s_tail, 16)
            sp.dma_start(w1[:, :, :], t_["W_top1"][0:3 * P, :].rearrange("(k p) n -> p k n", p=P)
                         ).then_inc(s_tail, 16)
            sp.dma_start(w1d[:, :], t_["W_top1"][3 * P:3 * P + DENSE, :]).then_inc(s_tail, 16)
            sp.dma_start(w2[:, :, :], t_["W_top2"].rearrange("(k p) n -> p k n", p=P)).then_inc(s_tail, 16)
            sp.dma_start(w3[:, :], t_["w3"]).then_inc(s_tail, 16)
            sp.dma_start(b1[:, :], t_["b1"]).then_inc(s_tail, 16)
            sp.dma_start(b2[:, :], t_["b2"]).then_inc(s_tail, 16)
            sp.dma_start(dense[:, :], t_["dense"]).then_inc(s_tail, 16)

            def replicate(t, q):
                sp.wait_ge(s_x1, t * CHUNKS + q + 1)
                for g in range(HG):
                    for r in range(R):
                        sp.dma_start(u[32 * r:32 * r + 32, q, g, :],
                                     xh[32 * g:32 * g + 32, q * CH:(q + 1) * CH]).then_inc(s_copies[q], 16)

            sp.wait_ge(s_k1l, 5)
            sp.wait_ge(s_k0w, 1)
            sp.wait_ge(s_gather, M * 16)
            sp.dma_start(ids_now[:, :], ids_h[P:2 * P, :]).then_inc(s_ids, 16)
            for q in range(CHUNKS):
                replicate(0, q)
            with sp.Fori(1, TILES - 1) as t:
                sp.wait_ge(s_gather, t * (M * 16) + M * 16)
                sp.dma_start(ids_now[:, :], ids_h[bass.ds(t * P + P, P), :]).then_inc(s_ids, 16)
                sp.wait_ge(s_z3_ps, t)
                for q in range(CHUNKS):
                    replicate(t, q)
            sp.wait_ge(s_z3_ps, TILES - 1)
            for q in range(CHUNKS):
                replicate(TILES - 1, q)
            sp.wait_ge(s_y, 1)
            sp.dma_start(t_["out"], y[:, :]).then_inc(s_out, 16)
            sp.wait_ge(s_out, 16)

        @block.gpsimd
        def _(pool):
            def gather(t):
                wait_alone(pool, s_ids, (t + 1) * 16)
                for m in range(M):
                    nc.gpsimd.indirect_dma_start(
                        emb[:, m * D:(m + 1) * D], None, t_[f"tbl_{m}"],
                        bass.IndirectOffsetOnAxis(ap=ids_now[:, m:m + 1], axis=0)).then_inc(s_gather, 16)

            def low_parts(t):
                for v in range(HALVES):
                    n = pool_cols(v) * CH
                    if not n:
                        continue
                    pool.wait_ge(s_hi, t * HALVES + v + 1)
                    if v >= RING:
                        wait_alone(pool, s_mm2, t * HALVES + v - RING + 1)
                    nc.gpsimd.tensor_tensor(prod_lo[:, v % RING, 0:n], prod[:, v % RING, 0:n],
                                            prod_hi[:, v % RING, 0:n].bitcast(F32),
                                            ALU.subtract).then_inc(s_lo_pool, 1)

            gather(0)
            with pool.Fori(0, TILES - 1) as t:
                wait_alone(pool, s_rest, t + 1)
                gather(t + 1)
                low_parts(t)
            low_parts(TILES - 1)

        @block.scalar
        def _(act):
            act.sem_inc(s_z3, 1)
            act.wait_ge(s_const, 32)
            nc.scalar.copy(ident_b[:, :], ident[:, :])
            nc.scalar.copy(sel[:, :], consts[0:XK, 0:SEL_N])
            nc.scalar.copy(rot[:, :], consts[0:XK, SEL_N:SEL_N + ROT_N])
            nc.scalar.copy(pick[:, :], consts[0:XK, SEL_N + ROT_N:SEL_N + ROT_N + M]).then_inc(s_sel, 1)
            act.wait_ge(s_k1, 16)
            k1h_f = k1h[:, :, :, :].rearrange("p j g o -> p (j g o)")
            for i in range(5):
                n = MJ * HG * H // 5
                nc.scalar.copy(k1h_f[:, i * n:(i + 1) * n], k1_raw_all[:, i * n:(i + 1) * n]).then_inc(s_k1h, 1)
            with act.Fori(0, TILES) as t:
                emb_dm = emb[:, :].rearrange("p (m d) -> p d m", m=M)
                act.wait_ge(s_gather, (t + 1) * (M * 16))
                nc.scalar.copy(parts[:, :, 0:M], emb_dm).then_inc(s_part0, 1)
                act.wait_ge(s_rest, t + 1)
                nc.scalar.copy(parts[:, :, M:2 * M], rest[:, :, :]).then_inc(s_part1, 1)
                x0_db = x0s[:, :].rearrange("p (b d) -> p d b", d=D)
                for i in range(D // DQ):
                    act.wait_ge(s_turned, t * (D // DQ) + i + 1)
                    nc.scalar.copy(x0_db[:, i * DQ:(i + 1) * DQ, :],
                                   ps_b[i % 2][:, 0:DQ * P].rearrange("p (d b) -> p d b", d=DQ)).then_inc(s_x0s, 1)
                for q in range(CHUNKS):
                    act.wait_ge(s_u1_ps, t * CHUNKS + q + 1)
                    nc.scalar.copy(u1[:, q * CH:(q + 1) * CH], ps[0:S_IN * M, XBANK + q % 2, :]).then_inc(s_u1, 1)
                for q in range(CHUNKS):
                    act.wait_ge(s_mm1, t * (CHUNKS * PAIRS) + (q + 1) * PAIRS)
                    nc.scalar.copy(xh[:, q * CH:(q + 1) * CH], ps[:, ACC + q % 2, :]).then_inc(s_x1, 1)
                for v in range(HALVES + LAG + 1):
                    if v < HALVES:
                        n = CH * sum(block_kind(v, i) != "R" for i in range(2))
                        act.wait_ge(s_p2, t * HALVES + v + 1)
                        if v >= RING:
                            wait_alone(act, s_mm2, t * HALVES + v - RING + 1)
                        nc.scalar.copy(prod_hi[:, v % RING, 0:n], prod[:, v % RING, 0:n]).then_inc(s_hi, 1)
                    q = (v - LAG) // (2 * UNITS)
                    if q >= 1 and (v - LAG) % (2 * UNITS) == 0:
                        if q == 1:
                            wait_alone(act, s_z1, t + 1)
                        act.wait_ge(s_mm2, t * HALVES + 2 * UNITS * q)
                        nc.scalar.copy(xh[:, (q - 1) * CH:q * CH], ps[:, ACC + (q - 1) % 2, :]).then_inc(s_x2, 1)
                for n in range(GROUPS + 1):
                    if n < GROUPS:
                        act.wait_ge(s_x2t_ps, t * GROUPS + n + 1)
                        if n >= 2:
                            wait_alone(act, s_g_ps, t * GROUPS + n - 1)
                        nc.scalar.copy(x2t[:, n % 2, :], ps[:, XBANK + n % 2, 0:P]).then_inc(s_x2t, 1)
                    if n >= 1:
                        k = n - 1
                        act.wait_ge(s_g_ps, t * GROUPS + k + 1)
                        nc.scalar.copy(gsb[:, :, k * GB:(k + 1) * GB].rearrange("p m b -> p b m"),
                                       ps[:, VBANK + k % 2, 0:GB * M].rearrange("p (b m) -> p b m", b=GB)
                                       ).then_inc(s_g, 1)
                wait_alone(act, s_z3_ps, t + 1)
                nc.scalar.copy(z[2][:, bass.ds(t * P, P)], ps[:, ACC, 0:P]).then_inc(s_z3, 1)
            act.wait_ge(s_tail, 10 * 16)
            for i in range(N1 // P):
                act.wait_ge(s_h1_ps, i + 1)
                nc.scalar.activation(h1[:, i, :], ps[:, VBANK + i, :], ACT.Relu, bias=b1[:, i:i + 1]).then_inc(s_h1, 1)
            for i in range(N2 // P):
                act.wait_ge(s_h2_ps, i + 1)
                nc.scalar.activation(h2[:, i, :], ps[:, XBANK + i, :], ACT.Relu, bias=b2[:, i:i + 1]).then_inc(s_h2, 1)
            act.wait_ge(s_y_ps, 1)
            nc.scalar.copy(y[:, :], ps[0:1, ACC, :]).then_inc(s_y, 1)

        @block.vector
        def _(dve):
            dve.wait_ge(s_k0, 32)
            nc.vector.tensor_tensor(k0w[:, :, :].rearrange("p k o -> p (k o)"),
                                    k0w[:, :, :].rearrange("p k o -> p (k o)"), k0_turned,
                                    ALU.add).then_inc(s_k0w, 1)
            k1h_f = k1h[:, :, :, :].rearrange("p j g o -> p (j g o)")
            k1l_f = k1l[:, :, :, :].rearrange("p j g o -> p (j g o)")
            for i in range(5):
                n = MJ * HG * H // 5
                dve.wait_ge(s_k1h, i + 1)
                nc.vector.tensor_tensor(k1l_f[:, i * n:(i + 1) * n], k1_raw_all[:, i * n:(i + 1) * n],
                                        k1h_f[:, i * n:(i + 1) * n].bitcast(F32), ALU.subtract).then_inc(s_k1l, 1)
            with dve.Fori(0, TILES) as t:
                emb_dm = emb[:, :].rearrange("p (m d) -> p d m", m=M)
                dve.wait_ge(s_part0, t + 1)
                nc.vector.tensor_tensor(rest[:, :, :], emb_dm, parts[:, :, 0:M], ALU.subtract).then_inc(s_rest, 1)
                dve.wait_ge(s_part1, t + 1)
                nc.vector.tensor_tensor(parts[:, :, 2 * M:3 * M], rest[:, :, :], parts[:, :, M:2 * M],
                                        ALU.subtract).then_inc(s_parts, 1)
                for i in range(CHUNKS * PAIRS):
                    q, k = divmod(i, PAIRS)
                    n = min(2, K1B - 2 * k)
                    dve.wait_ge(s_v1, t * (CHUNKS * PAIRS) + i + 1)
                    if k == 0:
                        wait_alone(dve, s_u1, t * CHUNKS + q + 1)
                    if i >= 2:
                        wait_alone(dve, s_mm1, t * (CHUNKS * PAIRS) + i - 1)
                    nc.vector.tensor_tensor(
                        prod[0:S_IN * M, i % 2, :].rearrange("p (a n) -> p a n", a=2)[:, 0:n, :],
                        u1[:, q * CH:(q + 1) * CH].unsqueeze(1).to_broadcast([S_IN * M, n, CH]),
                        ps[0:S_IN * M, VBANK + 2 * (i % 2):VBANK + 2 * (i % 2) + n, :],
                        ALU.mult).then_inc(s_p1, 1)
                wait_alone(dve, s_x1, t * CHUNKS + CHUNKS)
                nc.vector.tensor_reduce(z[0][:, bass.ds(t * P, P)],
                                        xh[:, :].rearrange("p (b d) -> p b d", d=D), AX.X, ALU.add).then_inc(s_z1, 1)
                for v in range(HALVES + 2):
                    if v < HALVES:
                        c, w = divmod(v, 2 * UNITS)
                        unit = v // 2
                        if w == 0:
                            wait_alone(dve, s_copies[c], (t + 1) * (16 * HG * R))
                        if v % 2 == 0:
                            wait_alone(dve, s_v2, t * (UNITS * CHUNKS) + unit + 1)
                        if v < RING:
                            if v < 2:
                                wait_alone(dve, s_mm1, (t + 1) * (CHUNKS * PAIRS) + v - 1)
                        else:
                            wait_alone(dve, s_hi, t * HALVES + v - RING + 1)
                            if pool_cols(v - RING):
                                wait_alone(dve, s_lo_pool, t * pool_ops(HALVES - 1) + pool_ops(v - RING))
                            if dve_ops(v - RING) > (dve_ops(v - RING - 1) if v > RING else 0):
                                wait_alone(dve, s_lo_dve, t * dve_ops(HALVES - 1) + dve_ops(v - RING))
                            if has_raw(v - RING):
                                wait_alone(dve, s_raw, t * raw_ops(HALVES - 1) + raw_ops(v - RING))
                        g0 = 2 * (v % 2)
                        nc.vector.tensor_tensor(
                            prod[:, v % RING, :].rearrange("p (g n) -> p g n", g=2),
                            u[:, c, g0:g0 + 2, :],
                            ps[:, VBANK + unit % VB, :].unsqueeze(1).to_broadcast([P, 2, CH]),
                            ALU.mult).then_inc(s_p2, 1)
                    w = v - 2
                    if w >= 0:
                        for i in range(2):
                            if block_kind(w, i) == "D":
                                dve.wait_ge(s_hi, t * HALVES + w + 1)
                                if w >= RING:
                                    wait_alone(dve, s_mm2, t * HALVES + w - RING + 1)
                                cols = slice(i * CH, (i + 1) * CH)
                                nc.vector.tensor_tensor(prod_lo[:, w % RING, cols], prod[:, w % RING, cols],
                                                        prod_hi[:, w % RING, cols].bitcast(F32),
                                                        ALU.subtract).then_inc(s_lo_dve, 1)
                if True:
                    dve.wait_ge(s_tail, 10 * 16)
                for n in range(GROUPS):
                    dve.wait_ge(s_x0t_ps, t * GROUPS + n + 1)
                    if n >= 2:
                        wait_alone(dve, s_g_ps, t * GROUPS + n - 1)
                    nc.vector.tensor_tensor(diag[:, n % 2, :, :],
                                            ps[:, VBANK + 2 + n % 2, 0:M].unsqueeze(1).to_broadcast([P, GB, M]),
                                            mask[:, :].unsqueeze(2).to_broadcast([P, GB, M]),
                                            ALU.mult).then_inc(s_diag, 1)
                wait_alone(dve, s_x2, t * CHUNKS + CHUNKS)
                nc.vector.tensor_reduce(z[1][:, bass.ds(t * P, P)],
                                        xh[:, :].rearrange("p (b d) -> p b d", d=D), AX.X, ALU.add).then_inc(s_z2, 1)

        @block.tensor
        def _(pe):
            pe.wait_ge(s_sel, 1)
            pe.wait_ge(s_k0w, 1)
            with pe.Fori(0, TILES) as t:
                for i in range(D // DQ):
                    if i == 0:
                        pe.wait_ge(s_parts, t + 1)
                    if i >= 2:
                        pe.wait_ge(s_x0s, t * (D // DQ) + i - 1)
                    for d in range(DQ):
                        last = nc.tensor.transpose(ps_b[i % 2][:, d * P:(d + 1) * P], parts[:, i * DQ + d, :],
                                                   ident_b[:, :])
                    last.then_inc(s_turned, 1)

                def three_copies(q):
                    if q == 0:
                        pe.wait_ge(s_x0s, (t + 1) * (D // DQ))
                    if q >= 2:
                        pe.wait_ge(s_u1, t * CHUNKS + q - 1)
                    nc.tensor.matmul(ps[0:S_IN * M, XBANK + q % 2, :], rot[:, K1B * S_IN * M:], x0s[:, q * CH:(q + 1) * CH],
                                     start=True, stop=True).then_inc(s_u1_ps, 1)

                def rotated(i):
                    q, k = divmod(i, PAIRS)
                    if i == 0:
                        pe.wait_ge(s_z3, t + 1)
                    if i >= 2:
                        pe.wait_ge(s_p1, t * (CHUNKS * PAIRS) + i - 1)
                    for a in range(min(2, K1B - 2 * k)):
                        kb = 2 * k + a
                        last = nc.tensor.matmul(ps[0:S_IN * M, VBANK + 2 * (i % 2) + a, :],
                                                rot[:, kb * S_IN * M:(kb + 1) * S_IN * M],
                                                x0s[:, q * CH:(q + 1) * CH], start=True, stop=True)
                    last.then_inc(s_v1, 1)

                def layer1(i):
                    q, k = divmod(i, PAIRS)
                    if k == 0 and q >= 2:
                        pe.wait_ge(s_x1, t * CHUNKS + q - 1)
                    pe.wait_ge(s_p1, t * (CHUNKS * PAIRS) + i + 1)
                    for a in range(min(2, K1B - 2 * k)):
                        kb = 2 * k + a
                        last = nc.tensor.matmul(ps[:, ACC + q % 2, :], k0w[:, kb, :],
                                                prod[0:S_IN * M, i % 2, a * CH:(a + 1) * CH],
                                                start=(kb == 0), stop=(kb == K1B - 1))
                    last.then_inc(s_mm1, 1)

                for i in range(CHUNKS * PAIRS + 1):
                    if i < CHUNKS:
                        three_copies(i)
                    if i < CHUNKS * PAIRS:
                        rotated(i)
                    if i >= 1:
                        layer1(i - 1)

                def broadcast(unit):
                    if unit == 0:
                        pe.wait_ge(s_p1, (t + 1) * (CHUNKS * PAIRS))
                    if unit >= VB:
                        pe.wait_ge(s_p2, t * HALVES + 2 * (unit - VB) + 2)
                    q, j = divmod(unit, UNITS)
                    nc.tensor.matmul(ps[:, VBANK + unit % VB, :], sel[:, j * P:(j + 1) * P],
                                     x0s[:, q * CH:(q + 1) * CH], start=True, stop=True).then_inc(s_v2, 1)

                def layer2_raw(v):
                    q, w = divmod(v, 2 * UNITS)
                    pe.wait_ge(s_p2, t * HALVES + v + 1)
                    for i in range(2):
                        if block_kind(v, i) == "R":
                            nc.tensor.matmul(ps[:, ACC + q % 2, :], k1raw[:, RAWJ.index(w // 2), :],
                                             prod[:, v % RING, i * CH:(i + 1) * CH],
                                             start=False, stop=False).then_inc(s_raw, 1)

                def layer2(v):
                    q, w = divmod(v, 2 * UNITS)
                    j, g0 = w // 2, 2 * (w % 2)
                    if w == 0:
                        if q < 2:
                            pe.wait_ge(s_x1, t * CHUNKS + q + 3)
                        else:
                            pe.wait_ge(s_x2, t * CHUNKS + q - 1)
                    pe.wait_ge(s_hi, t * HALVES + v + 1)
                    if pool_cols(v):
                        pe.wait_ge(s_lo_pool, t * pool_ops(HALVES - 1) + pool_ops(v))
                    if any(block_kind(v, i) == "D" for i in range(2)):
                        pe.wait_ge(s_lo_dve, t * dve_ops(HALVES - 1) + dve_ops(v))
                    for i in range(2):
                        if block_kind(v, i) == "R":
                            continue
                        cols = slice(i * CH, (i + 1) * CH)
                        for n, (w_, x_) in enumerate(((k1h, prod_hi), (k1h, prod_lo), (k1l, prod_hi))):
                            final = w == 2 * UNITS - 1 and n == 2 and all(
                                block_kind(v, x) == "R" for x in range(i + 1, 2))
                            last = nc.tensor.matmul(ps[:, ACC + q % 2, :], w_[:, j, g0 + i, :], x_[:, v % RING, cols],
                                                    start=(w == 0 and i == 0 and n == 0), stop=final)
                    last.then_inc(s_mm2, 1)

                if True:
                    pe.wait_ge(s_k1l, 5)
                    pe.wait_ge(s_tail, 10 * 16)
                broadcast(0)
                for v in range(HALVES + LAG):
                    unit = v // 2 + 1
                    if v % 2 == 0 and unit < UNITS * CHUNKS:
                        broadcast(unit)
                    if v >= LAG:
                        layer2(v - LAG)
                    if 0 <= v - RAW_LAG < HALVES and has_raw(v - RAW_LAG):
                        layer2_raw(v - RAW_LAG)

                for n in range(GROUPS + 1):
                    if n < GROUPS:
                        cols = slice(n * GB * D, (n + 1) * GB * D)
                        if n == 0:
                            pe.wait_ge(s_x2, t * CHUNKS + CHUNKS)
                        if n >= 2:
                            pe.wait_ge(s_x2t, t * GROUPS + n - 1)
                            pe.wait_ge(s_diag, t * GROUPS + n - 1)
                        nc.tensor.transpose(ps[:, XBANK + n % 2, 0:P], xh[:, cols],
                                            ident[:, :]).then_inc(s_x2t_ps, 1)
                        nc.tensor.matmul(ps[:, VBANK + 2 + n % 2, 0:M], x0s[:, cols], pick[:, :],
                                         start=True, stop=True).then_inc(s_x0t_ps, 1)
                    if n >= 1:
                        k = n - 1
                        pe.wait_ge(s_x2t, t * GROUPS + k + 1)
                        pe.wait_ge(s_diag, t * GROUPS + k + 1)
                        if k >= 2:
                            pe.wait_ge(s_g, t * GROUPS + k - 1)
                        nc.tensor.matmul(ps[:, VBANK + k % 2, 0:GB * M], x2t[:, k % 2, :],
                                         diag[:, k % 2, :, :].rearrange("p b m -> p (b m)"),
                                         start=True, stop=True).then_inc(s_g_ps, 1)
                pe.wait_ge(s_g, t * GROUPS + GROUPS)
                for m in range(M):
                    last = nc.tensor.matmul(ps[:, ACC, 0:P], k2w[:, m, :], gsb[:, m, :],
                                            start=(m == 0), stop=(m == M - 1))
                last.then_inc(s_z3_ps, 1)

            pe.wait_ge(s_z3, TILES + 1)
            pe.wait_ge(s_z1, TILES)
            pe.wait_ge(s_z2, TILES)
            for i in range(N1 // P):
                for k in range(3):
                    nc.tensor.matmul(ps[:, VBANK + i, :], w1[:, k, i * P:(i + 1) * P], z[k][:, :],
                                     start=(k == 0), stop=False)
                nc.tensor.matmul(ps[:, VBANK + i, :], w1d[:, i * P:(i + 1) * P], dense[:, :],
                                 start=False, stop=True).then_inc(s_h1_ps, 1)
            for i in range(N2 // P):
                for k in range(N1 // P):
                    pe.wait_ge(s_h1, k + 1)
                    last = nc.tensor.matmul(ps[:, XBANK + i, :], w2[:, k, i * P:(i + 1) * P], h1[:, k, :],
                                            start=(k == 0), stop=(k == N1 // P - 1))
                last.then_inc(s_h2_ps, 1)
            for k in range(N2 // P):
                pe.wait_ge(s_h2, k + 1)
                last = nc.tensor.matmul(ps[0:1, ACC, :], w3[:, k:k + 1], h2[:, k, :],
                                        start=(k == 0), stop=(k == N2 // P - 1))
            last.then_inc(s_y_ps, 1)


def lay_out(inputs):
    import numpy as np

    a = {f"tbl_{m}": inputs[f"tbl_{m}"] for m in range(M)}
    a["ids"] = inputs["ids"]
    a["dense"] = inputs["dense_ctx"].T
    k0 = inputs["L0_rec_k0"].transpose(1, 2, 0)
    straight = np.zeros((S_IN * M, K1B, H), k0.dtype)
    turned = np.zeros((S_IN * M, K1B, H), k0.dtype)
    fields = np.arange(M)
    for s in range(SHIFTS):
        k, i = divmod(s, S_IN)
        other = (fields + s) % M
        straight[i * M:(i + 1) * M, k] = k0[fields, other]
        if 0 < s < M // 2:
            turned[i * M:(i + 1) * M, k] = k0[other, fields]
    a["k0_straight"] = straight
    a["k0_turned"] = turned.reshape(S_IN * M, K1B * H)
    k1 = inputs["L0_rec_k1"].reshape(H, HG, 32, MJ, R)
    a["k1"] = k1.transpose(4, 2, 3, 1, 0).reshape(P, MJ * HG * H)
    a["k2"] = inputs["L0_rec_k2"].transpose(1, 2, 0)
    a["W_top1"] = inputs["W_top1"]
    a["W_top2"] = inputs["W_top2"]
    a["w3"] = inputs["W_top3"].reshape(N2 // P, P).T
    a["b1"] = inputs["b_top1"].reshape(N1 // P, P).T
    a["b2"] = inputs["b_top2"].reshape(N2 // P, P).T
    m_of = np.arange(XK) % M
    sel = (m_of[:, None] == (np.arange(MJ)[:, None] * R + np.arange(P)[None, :] // 32).reshape(-1)[None, :])
    rows = np.arange(S_IN * M)
    shift = [(rows % M + k * S_IN + rows // M) % M for k in range(K1B)] + [rows % M]
    rot = m_of[:, None] == np.concatenate(shift)[None, :]
    pick = m_of[:, None] == fields[None, :]
    a["consts"] = np.concatenate([sel, rot, pick], axis=1).astype(np.float32)
    a["ident"] = np.eye(P, dtype=np.float32)
    a["mask"] = (np.arange(P)[:, None] // D == np.arange(GB)[None, :]).astype(np.float32)
    return {k: np.ascontiguousarray(v) for k, v in a.items()}


def kernel(**inputs):
    import numpy as np
    import concourse.bacc as bacc
    from concourse.bass_utils import run_bass_kernel_spmd

    nc = bacc.Bacc("TRN2", target_bir_lowering=False, num_devices=1)
    laid = lay_out({k: np.asarray(v) for k, v in inputs.items()})
    tensors = {k: nc.dram_tensor(f"in_{k}", v.shape, mybir.dt.from_np(v.dtype), kind="ExternalInput").ap()
               for k, v in laid.items()}
    out = nc.dram_tensor("out_y", (B, 1), F32, kind="ExternalOutput").ap()
    tensors["out"] = out.rearrange("b o -> o b")
    build(nc, tensors)
    r = run_bass_kernel_spmd(nc, [{f"in_{k}": v for k, v in laid.items()}], core_ids=[0])
    return r.results[0]["out_y"]
```

```python
from contextlib import ExitStack

import concourse.bass as bass
from concourse import mybir

F32 = mybir.dt.float32
F32R = mybir.dt.float32r
BF16 = mybir.dt.bfloat16
I32 = mybir.dt.int32
ALU = mybir.AluOpType
ACT = mybir.ActivationFunctionType
AX = mybir.AxisListType

B = 512
M = 40
D = 16
H = 128
DENSE = 16
N1, N2 = 512, 256

P = 128
TILES = B // P
CH = 512
CHUNKS = D * P // CH
GB = P // D
NG = CH // P
TG = NG * CHUNKS
DT = 8
PARTS = 3
XK = PARTS * M

SHIFTS = M // 2 + 1
S_IN = P // M
KP = S_IN * M
K1B = SHIFTS // S_IN
P1_RING = 4

R = 4
BLOCKS = M // R
SLOTS = NG * BLOCKS
TSLOTS = CHUNKS * SLOTS
SHARE_GATHERING, SHARE_REST = "YZYZYZYZYZ", "ZYZYZZYZYZ"
GATHERING = 8
GATHER_AT = [m * 5 // 2 for m in range(M)]
BLK_BANKS = 4
TMP_RING = 4
ACC = 2

AT_U1, AT_PICK = 1, 8
AT_V = [3 + 4 * i for i in range(K1B)]
MM_LAG = 4
AT_X1 = 36
AT_G = 5
AT_FINAL = 3
AT_TURN = (36, 39)
AT_SPLIT = 26
AT_L3 = 26
L3_STEP = 5
AT_L3_END = AT_L3 + M // L3_STEP

FIRST = 32
WARM = 30

LAG = 2 * GB

BASE = 64


def share(k):
    return (SHARE_GATHERING if k % TSLOTS < GATHERING * BLOCKS else SHARE_REST)[k % BLOCKS]


def count(kind, k):
    if k < 0:
        return count(kind, k + TSLOTS) - count(kind, TSLOTS - 1)
    return sum(share(x) == kind for x in range(k + 1))


def adds(k):
    if k < 0:
        return adds(k + TSLOTS) - adds(TSLOTS - 1)
    return sum(share(x) == "Z" and not first_of(x) for x in range(k + 1))


def first_of(k):
    return share(k) not in [share(x) for x in range(k // BLOCKS * BLOCKS, k)]


NY, NZ, NADD = count("Y", TSLOTS - 1), count("Z", TSLOTS - 1), adds(TSLOTS - 1)


def misc_items(q, last):
    items = [(AT_G + BLOCKS * n, "G", n) for n in range(NG)]
    if not (last and q == CHUNKS - 1):
        items += [(AT_U1, "U1", 0), (AT_PICK, "PICK", 0)]
    if q == CHUNKS - 2 and not last:
        items += [(at, "T", i) for i, at in enumerate(AT_TURN)]
    return sorted(items)


MISC0 = 2
NMISC = sum(len(misc_items(q, False)) for q in range(CHUNKS))

assert NADD % TMP_RING == 0 and TSLOTS % BLK_BANKS == 0 and CHUNKS * K1B % P1_RING == 0


def misc_of(q, what, i, last):
    before = sum(len(misc_items(x, last)) for x in range(q))
    return before + [x[1:] for x in misc_items(q, last)].index((what, i))


def build(nc, t_):
    ctx = ExitStack()
    with ctx:
        def sb(name, shape, dt=F32):
            return ctx.enter_context(nc.sbuf_tensor(name, shape, dt))

        ids_now = sb("ids_now", [P, M], I32)
        emb = sb("emb", [P, M * D])
        rest = sb("rest", [P, D, M])
        parts = sb("parts", [P, D, XK], BF16)
        x0s = sb("x0s", [XK, CHUNKS * CH], BF16)
        x0t = sb("x0t", [P, 2, NG, M])
        u1 = sb("u1", [KP, CH])
        p1 = sb("p1", [KP, P1_RING, CH])
        x1h = sb("x1h", [H, 2, CH], F32R)
        x1l = sb("x1l", [H, 2, CH], F32R)
        acc = sb("acc", [P, 2, ACC + R, H])
        tmp_z = sb("tmp_z", [P, TMP_RING, R, H])
        x2t = sb("x2t", [P, 2, H])
        diag = sb("diag", [P, 2, GB, M + 1])
        mask = sb("mask", [P, GB])
        gsb = sb("gsb", [H, M + 1, P + LAG])
        k1h = sb("k1h", [H, M, H], F32R)
        k1l = sb("k1l", [H, M, H], F32R)
        k1raw = sb("k1raw", [H, M, H])
        k2w = sb("k2w", [H, M, H])
        k0w = sb("k0w", [KP, K1B, H])
        k0_turned = sb("k0_turned", [KP, K1B * H])
        rot = sb("rot", [XK, (K1B + 1) * KP], BF16)
        pick = sb("pick", [XK, M], BF16)
        ident_b = sb("ident_b", [P, P], BF16)
        ROT_N = (K1B + 1) * KP
        consts = sb("consts", [P, ROT_N + M + P])
        z1 = sb("z1", [P, B])
        z2 = sb("z2", [P, LAG + B])
        z3 = sb("z3", [P, LAG + B])
        dense = sb("dense", [DENSE, B])
        w1 = sb("w1", [P, 3, N1])
        w1d = sb("w1d", [DENSE, N1])
        w2 = sb("w2", [P, N1 // P, N2])
        w3 = sb("w3", [P, N2 // P])
        b1 = sb("b1", [P, N1 // P])
        b2 = sb("b2", [P, N2 // P])
        h1 = sb("h1", [P, N1 // P, B])
        h2 = sb("h2", [P, N2 // P, B])
        y = sb("y", [1, B])

        ps = ctx.enter_context(nc.psum_tensor("ps", [P, 8, CH], F32))
        ACC1, VB, MISC = 4, 5, 7
        L3_BANK = VB + 1
        H1_BANKS, H2_BANKS, Y_BANK = (ACC1, VB, VB + 1, 0), (1, 2), 3

        def sem(name):
            return ctx.enter_context(nc.semaphore(name))

        s_ids = sem("s_ids")
        s_const = sem("s_const")
        s_k0 = sem("s_k0")
        s_k1 = sem("s_k1")
        s_mask = sem("s_mask")
        s_tail = sem("s_tail")
        s_first = sem("s_first")
        s_gather = sem("s_gather")
        s_out = sem("s_out")
        s_sel = sem("s_sel")
        s_k1h = sem("s_k1h")
        s_k1l = sem("s_k1l")
        s_k0w = sem("s_k0w")
        s_zero = sem("s_zero")
        s_turned = sem("s_turned")
        s_x0s = sem("s_x0s")
        s_h1_ps, s_h1, s_h2_ps, s_h2, s_y_ps, s_y = (sem(x) for x in ("s_h1_ps", "s_h1", "s_h2_ps", "s_h2", "s_y_ps", "s_y"))
        s_part0 = sem("s_part0")
        s_rest = sem("s_rest")
        s_part1 = sem("s_part1")
        s_parts = sem("s_parts")
        s_misc = sem("s_misc")
        s_took = sem("s_took")
        s_v = sem("s_v")
        s_p1 = sem("s_p1")
        s_mm1 = sem("s_mm1")
        s_x1h = sem("s_x1h")
        s_x1l = sem("s_x1l")
        s_z1 = sem("s_z1")
        s_blk = sem("s_blk")
        s_y4 = sem("s_y4")
        s_z4 = sem("s_z4")
        s_add = sem("s_add")
        s_x2t = sem("s_x2t")
        s_diag = sem("s_diag")
        s_l3 = sem("s_l3")
        s_z3 = sem("s_z3")
        s_z2 = sem("s_z2")
        passed = sem("passed")

        def wait_alone(eng, s, value):
            eng.wait_ge(s, value)
            eng.sem_inc(passed, 1)

        def misc_count(t, q, what, i, last):
            return t * NMISC + (BASE + MISC0 + misc_of(q, what, i, last) + 1)

        def gathered(t):
            return t * (M * 16) + (M - FIRST) * 16

        def split_range(part):
            return (slice(0, FIRST), slice(FIRST, M), slice(0, M))[part]

        def tile_loop(eng, body):
            with eng.Fori(0, TILES - 1) as t:
                body(t, False)
            body(TILES - 1, True)

        block = ctx.enter_context(nc.Block())

        @block.sync
        def _(sp):
            def load(out, name, s):
                sp.dma_start(out, t_[name]).then_inc(s, 16)

            sp.dma_start(ids_now[:, :], t_["ids"][0:P, :]).then_inc(s_ids, 16)
            load(consts[:, :], "consts", s_const)
            load(k0w[:, :, :], "k0_straight", s_k0)
            load(k0_turned[:, :], "k0_turned", s_k0)
            load(mask[:, :], "mask", s_mask)
            load(k1raw[:, :, :], "k1", s_k1)
            load(k2w[:, :, :], "k2", s_tail)
            sp.dma_start(w1[:, :, :], t_["W_top1"][0:3 * P, :].rearrange("(k p) n -> p k n", p=P)
                         ).then_inc(s_tail, 16)
            sp.dma_start(w1d[:, :], t_["W_top1"][3 * P:3 * P + DENSE, :]).then_inc(s_tail, 16)
            sp.dma_start(w2[:, :, :], t_["W_top2"].rearrange("(k p) n -> p k n", p=P)).then_inc(s_tail, 16)
            load(w3[:, :], "w3", s_tail)
            load(b1[:, :], "b1", s_tail)
            load(b2[:, :], "b2", s_tail)
            load(dense[:, :], "dense", s_tail)
            sp.wait_ge(s_first, FIRST * 16)
            with sp.Fori(1, TILES) as t:
                sp.wait_ge(s_gather, t * (M * 16) - FIRST * 16)
                sp.dma_start(ids_now[:, :], t_["ids"][bass.ds(t * P, P), :]).then_inc(s_ids, 16)
            sp.wait_ge(s_y, 1)
            sp.dma_start(t_["out"], y[:, :]).then_inc(s_out, 16)
            sp.wait_ge(s_out, 16)

        @block.gpsimd
        def _(pool):
            pool.sem_inc(s_add, BASE)

            def gather(m, s):
                nc.gpsimd.indirect_dma_start(
                    emb[:, m * D:(m + 1) * D], None, t_[f"tbl_{m}"],
                    bass.IndirectOffsetOnAxis(ap=ids_now[:, m:m + 1], axis=0)).then_inc(s, 16)

            def tile(t, last):
                for k in range(TSLOTS):
                    if share(k) == "Z" and not first_of(k):
                        n = k // BLOCKS
                        wait_alone(pool, s_z4, t * NZ + (BASE + count("Z", k)))
                        wait_alone(pool, s_add, t * NADD + (BASE + adds(k) - 1))
                        nc.gpsimd.tensor_tensor(acc[:, n % 2, ACC:, :], acc[:, n % 2, ACC:, :],
                                                tmp_z[:, (adds(k) - 1) % TMP_RING, :, :],
                                                ALU.add).then_inc(s_add, 1)
                    if not last and k in GATHER_AT:
                        if k == 0:
                            wait_alone(pool, s_ids, (t + 2) * 16)
                            wait_alone(pool, s_rest, t + (BASE + 1))
                        gather(GATHER_AT.index(k), s_gather)

            pool.wait_ge(s_ids, 16)
            for m in range(M):
                gather(m, s_first if m < FIRST else s_gather)
            tile_loop(pool, tile)

        @block.scalar
        def _(act):
            for s in (s_took, s_x1h, s_z4, s_z2, s_z3):
                act.sem_inc(s, BASE)
            for s in (s_part0, s_part1):
                act.sem_inc(s, BASE - 1)
            act.wait_ge(s_const, 16)
            nc.scalar.copy(rot[:, :], consts[0:XK, 0:ROT_N])
            nc.scalar.copy(pick[:, :], consts[0:XK, ROT_N:ROT_N + M])
            nc.scalar.copy(ident_b[:, :], consts[:, ROT_N + M:ROT_N + M + P]).then_inc(s_sel, 1)
            act.wait_ge(s_k1, 16)
            for i in range(5):
                m = slice(i * M // 5, (i + 1) * M // 5)
                nc.scalar.copy(k1h[:, m, :], k1raw[:, m, :]).then_inc(s_k1h, 1)

            emb_dm = emb[:, :].rearrange("p (m d) -> p d m", m=M)
            x0_db = x0s[:, :].rearrange("p (b d) -> p d b", d=D)

            def split0(t, part=2):
                act.wait_ge(s_gather, gathered(t)) if part else act.wait_ge(s_first, FIRST * 16)
                m = split_range(part)
                nc.scalar.copy(parts[:, :, m], emb_dm[:, :, m]).then_inc(s_part0, 1)

            def split1(t, part=2):
                act.wait_ge(s_rest, t + (BASE + min(part, 1)))
                m = split_range(part)
                nc.scalar.copy(parts[:, :, M + m.start:M + m.stop], rest[:, :, m]).then_inc(s_part1, 1)

            def took_turned(i, bank, b, s):
                nc.scalar.copy(x0_db[:, i * DT:(i + 1) * DT, b],
                               ps[0:XK, bank, :].bitcast(BF16)[:, 0:DT * P].rearrange("p (d b) -> p d b", d=DT)[:, :, b]
                               ).then_inc(s, 1)

            def took_u1(c, value):
                wait_alone(act, s_p1, c * K1B + BASE)
                act.wait_ge(s_misc, value)
                nc.scalar.copy(u1[:, :], ps[0:KP, MISC, :]).then_inc(s_took, 1)

            def took_pick(slot, diag_value, value):
                wait_alone(act, s_diag, diag_value)
                act.wait_ge(s_misc, value)
                nc.scalar.copy(x0t[:, slot, :, :],
                               ps[:, MISC, 0:NG * M].rearrange("p (n m) -> p n m", m=M)).then_inc(s_took, 1)

            def contracted(place):
                nc.scalar.copy(gsb[:, :, place * GB:(place + 1) * GB].rearrange("p m b -> p b m"),
                               ps[:, MISC, 0:GB * (M + 1)].rearrange("p (b m) -> p b m", b=GB)).then_inc(s_took, 1)

            def lead_x1(c, slot):
                wait_alone(act, s_blk, (c - 1) * SLOTS + BASE)
                act.wait_ge(s_mm1, (c + 1) * K1B + BASE)
                nc.scalar.copy(x1h[:, slot, :], ps[:, ACC1, :]).then_inc(s_x1h, 1)

            def tile(t, last):
                for k in range(TSLOTS):
                    q, s = divmod(k, SLOTS)
                    c = t * CHUNKS + q
                    g, n, b = k // BLOCKS, s // BLOCKS, k % BLOCKS
                    if share(k) == "Z":
                        wait_alone(act, s_blk, t * TSLOTS + (BASE + k + 1))
                        if first_of(k):
                            wait_alone(act, s_x2t, t * TG + (BASE + g))
                            out = acc[:, g % 2, ACC:, :]
                        else:
                            wait_alone(act, s_add, t * NADD + (BASE + adds(k) - TMP_RING))
                            out = tmp_z[:, (adds(k) - 1) % TMP_RING, :, :]
                        for r in range(R):
                            m = R * b + r
                            last_ = nc.scalar.activation(out[:, r, :], ps[:, k % BLK_BANKS, r * H:(r + 1) * H],
                                                         ACT.Copy, scale=x0t[:, q % 2, n, m:m + 1])
                        last_.then_inc(s_z4, 1)
                    if q == CHUNKS - 2 and not last:
                        if s == AT_SPLIT:
                            split0(t + 1)
                        if s == AT_SPLIT + 4:
                            split1(t + 1)
                    if q == CHUNKS - 1 and s == AT_L3_END and not last:
                        act.wait_ge(s_l3, t + (BASE + 1))
                        nc.scalar.copy(z3[:, bass.ds(t * P, P)], ps[:, L3_BANK, 0:P]).then_inc(s_z3, 1)
                        nc.scalar.copy(z2[:, bass.ds(t * P, P)], gsb[:, M, 0:P]).then_inc(s_z2, 1)
                    if s == AT_X1 and not (last and q == CHUNKS - 1):
                        lead_x1(c + 1, (q + 1) % 2)
                    for at, what, i in misc_items(q, last):
                        if at != s:
                            continue
                        value = misc_count(t, q, what, i, last)
                        if what == "U1":
                            took_u1(c + 1, value)
                        if what == "PICK":
                            took_pick((q + 1) % 2, c * NG + BASE, value)
                        if what == "T":
                            act.wait_ge(s_misc, value)
                            took_turned(i, MISC, slice(0, P), s_took)
                        if what == "G":
                            wait_alone(act, s_z2, t + (BASE + (g == TG - 1 and not last)))
                            wait_alone(act, s_misc, value)
                            place = g + 1 if last else (g + 1) % TG
                            contracted(place)

            split0(0, 0)
            split1(0, 0)
            split0(0, 1)
            split1(0, 1)
            for i in range(D // DT):
                act.wait_ge(s_turned, i + 1)
                took_turned(i, i, slice(0, CH // D), s_x0s)
            took_u1(0, BASE + 1)
            took_pick(0, BASE, BASE + 2)
            for i in range(D // DT):
                took_turned(i, i, slice(CH // D, P), s_x0s)
            lead_x1(0, 0)
            tile_loop(act, tile)

            end = misc_count(TILES - 1, CHUNKS - 1, "G", NG - 1, True)
            act.wait_ge(s_misc, end + 1)
            contracted(TG + 1)
            act.wait_ge(s_took, end + 1)
            nc.scalar.copy(z2[:, (TILES - 1) * P:], gsb[:, M, :]).then_inc(s_z2, 1)
            act.wait_ge(s_misc, end + 2)
            nc.scalar.copy(z3[:, (TILES - 1) * P:], ps[:, MISC, 0:P + LAG]).then_inc(s_z3, 1)
            act.wait_ge(s_tail, 8 * 16)
            for i in range(N1 // P):
                act.wait_ge(s_h1_ps, i + 1)
                nc.scalar.activation(h1[:, i, :], ps[:, H1_BANKS[i], :], ACT.Relu, bias=b1[:, i:i + 1]).then_inc(s_h1, 1)
            for i in range(N2 // P):
                act.wait_ge(s_h2_ps, i + 1)
                nc.scalar.activation(h2[:, i, :], ps[:, H2_BANKS[i], :], ACT.Relu, bias=b2[:, i:i + 1]).then_inc(s_h2, 1)
            act.wait_ge(s_y_ps, 1)
            nc.scalar.copy(y[:, :], ps[0:1, Y_BANK, :]).then_inc(s_y, 1)

        @block.vector
        def _(dve):
            for s in (s_p1, s_x1l, s_z1, s_y4, s_x2t, s_diag):
                dve.sem_inc(s, BASE)
            for s in (s_rest, s_parts):
                dve.sem_inc(s, BASE - 1)
            for buf in (acc[:, 1, :, :], diag[:, 1, :, 0:M], gsb[:, :, 0:GB]):
                nc.vector.memset(buf, 0.0).then_inc(s_zero, 1)
            dve.wait_ge(s_mask, 16)
            for i in range(2):
                nc.vector.tensor_copy(diag[:, i, :, M], mask[:, :]).then_inc(s_zero, 1)
            dve.wait_ge(s_zero, 5)
            dve.wait_ge(s_k0, 32)
            k0_flat = k0w[:, :, :].rearrange("p k o -> p (k o)")
            nc.vector.tensor_tensor(k0_flat, k0_flat, k0_turned[:, :], ALU.add).then_inc(s_k0w, 1)
            for i in range(5):
                m = slice(i * M // 5, (i + 1) * M // 5)
                dve.wait_ge(s_k1h, i + 1)
                nc.vector.tensor_tensor(k1l[:, m, :], k1raw[:, m, :], k1h[:, m, :].bitcast(F32),
                                        ALU.subtract).then_inc(s_k1l, 1)

            emb_dm = emb[:, :].rearrange("p (m d) -> p d m", m=M)

            def split_rest(t, part=2):
                dve.wait_ge(s_part0, t + (BASE + min(part, 1)))
                m = split_range(part)
                nc.vector.tensor_tensor(rest[:, :, m], emb_dm[:, :, m], parts[:, :, m], ALU.subtract).then_inc(s_rest, 1)

            def split2(t, part=2):
                dve.wait_ge(s_part1, t + (BASE + min(part, 1)))
                m = split_range(part)
                nc.vector.tensor_tensor(parts[:, :, 2 * M + m.start:2 * M + m.stop], rest[:, :, m],
                                        parts[:, :, M + m.start:M + m.stop], ALU.subtract).then_inc(s_parts, 1)

            def pairs(c, q, i, u1_value):
                at = K1B * q + i
                wait_alone(dve, s_v, c * K1B + (BASE + i + 1))
                wait_alone(dve, s_mm1, c * K1B + (BASE + i + 1 - P1_RING))
                if i == 0:
                    wait_alone(dve, s_took, u1_value)
                nc.vector.tensor_tensor(p1[:, at % P1_RING, :], u1[:, :], ps[0:KP, VB + at % 2, :],
                                        ALU.mult).then_inc(s_p1, 1)

            def rest_x1(c, slot, cols):
                wait_alone(dve, s_x1h, c + (BASE + 1))
                nc.vector.tensor_tensor(x1l[:, slot, :], ps[:, ACC1, :], x1h[:, slot, :].bitcast(F32),
                                        ALU.subtract).then_inc(s_x1l, 1)
                nc.vector.tensor_reduce(z1[:, cols], ps[:, ACC1, :].rearrange("p (b d) -> p b d", d=D),
                                        AX.X, ALU.add).then_inc(s_z1, 1)

            def final(t, g, contracted):
                slot = (g - 1) % 2
                k = g * BLOCKS - 1
                wait_alone(dve, s_y4, t * (R * NY) + (BASE + R * count("Y", k)))
                wait_alone(dve, s_add, t * NADD + (BASE + adds(k)))
                wait_alone(dve, s_misc, contracted)
                nc.vector.tensor_reduce(x2t[:, slot, :], acc[:, slot, :, :].rearrange("p r h -> p h r"),
                                        AX.X, ALU.add).then_inc(s_x2t, 1)

            def tile(t, last):
                for k in range(TSLOTS):
                    q, s = divmod(k, SLOTS)
                    c = t * CHUNKS + q
                    g, n, b = k // BLOCKS, s // BLOCKS, k % BLOCKS

                    def contracted(x):
                        if x >= 0:
                            return misc_count(t, (x + 1) // NG, "G", (x + 1) % NG, last)
                        return misc_count(t - 1, (x + 1 + TG) // NG, "G", (x + 1 + TG) % NG, False)

                    if share(k) == "Y":
                        wait_alone(dve, s_blk, t * TSLOTS + (BASE + k + 1))
                        done = BASE + R * (count("Y", k) - 1)
                        if first_of(k):
                            wait_alone(dve, s_x2t, t * TG + (BASE + g))
                        for r in range(R):
                            m = R * b + r
                            out = acc[:, g % 2, r % ACC, :]
                            src = ps[:, k % BLK_BANKS, r * H:(r + 1) * H]
                            factor = x0t[:, q % 2, n, m:m + 1]
                            if first_of(k) and r < ACC:
                                nc.vector.tensor_scalar(out, src, factor, None, ALU.mult).then_inc(s_y4, 1)
                            else:
                                wait_alone(dve, s_y4, t * (R * NY) + (done + r - ACC + 1))
                                nc.vector.scalar_tensor_tensor(out=out, in0=src, scalar=factor, in1=out,
                                                               op0=ALU.mult, op1=ALU.add).then_inc(s_y4, 1)
                    if b == AT_FINAL:
                        final(t, g, contracted(g - 3))
                    if b == AT_G:
                        wait_alone(dve, s_misc, contracted(g - 2))
                        wait_alone(dve, s_blk, t * TSLOTS + (BASE + q * SLOTS + 1))
                        nc.vector.tensor_tensor(diag[:, g % 2, :, 0:M],
                                                x0t[:, q % 2, n, :].unsqueeze(1).to_broadcast([P, GB, M]),
                                                mask[:, :].unsqueeze(2).to_broadcast([P, GB, M]),
                                                ALU.mult).then_inc(s_diag, 1)
                    if not (last and q == CHUNKS - 1):
                        for i in range(K1B):
                            if s == AT_V[i] + 1:
                                pairs(c + 1, (q + 1) % CHUNKS, i, misc_count(t, q, "U1", 0, last))
                        if s == AT_X1 + 1:
                            rest_x1(c + 1, (q + 1) % 2, bass.ds((c + 1) * (CH // D), CH // D) if not last
                                    else slice((c + 1) * (CH // D), (c + 2) * (CH // D)))
                    if q == CHUNKS - 2 and not last:
                        if s == AT_SPLIT + 2:
                            split_rest(t + 1)
                        if s == AT_SPLIT + 6:
                            split2(t + 1)

            for part in range(2):
                split_rest(0, part)
                split2(0, part)
            for i in range(K1B):
                pairs(0, 0, i, BASE + 1)
            rest_x1(0, 0, slice(0, CH // D))
            tile_loop(dve, tile)
            final(TILES - 1, TG, misc_count(TILES - 1, (TG - 2) // NG, "G", (TG - 2) % NG, True))

        @block.tensor
        def _(pe):
            for s in (s_misc, s_v, s_mm1, s_blk, s_l3):
                pe.sem_inc(s, BASE)

            def bank_free(value):
                pe.wait_ge(s_took, value - 1)

            def turn(i, bank, s):
                out = ps[0:XK, bank, :].bitcast(BF16)
                for d in range(DT):
                    last = nc.tensor.transpose(out[:, d * P:(d + 1) * P], parts[:, i * DT + d, :], ident_b[:, :])
                last.then_inc(s, 1)

            def three_copies(q, value):
                bank_free(value)
                nc.tensor.matmul(ps[0:KP, MISC, :], rot[:, K1B * KP:(K1B + 1) * KP], x0s[:, q * CH:(q + 1) * CH],
                                 start=True, stop=True).then_inc(s_misc, 1)

            def turn_back(q, value):
                bank_free(value)
                for n in range(NG):
                    col = q * CH + n * P
                    last = nc.tensor.matmul(ps[:, MISC, n * M:(n + 1) * M], x0s[:, col:col + P], pick[:, :],
                                            start=True, stop=True)
                last.then_inc(s_misc, 1)

            def rotated(c, q, i):
                pe.wait_ge(s_p1, c * K1B + (BASE + i - 1))
                nc.tensor.matmul(ps[0:KP, VB + (K1B * q + i) % 2, :], rot[:, i * KP:(i + 1) * KP],
                                 x0s[:, q * CH:(q + 1) * CH], start=True, stop=True).then_inc(s_v, 1)

            def layer1(c, q, i):
                if i == 0:
                    pe.wait_ge(s_z1, c + BASE)
                pe.wait_ge(s_p1, c * K1B + (BASE + i + 1))
                nc.tensor.matmul(ps[:, ACC1, :], k0w[:, i, :], p1[:, (K1B * q + i) % P1_RING, :],
                                 start=(i == 0), stop=(i == K1B - 1)).then_inc(s_mm1, 1)

            def contract(g, x2t_value, diag_value, value):
                pe.wait_ge(s_x2t, x2t_value)
                pe.wait_ge(s_diag, diag_value)
                bank_free(value)
                nc.tensor.matmul(ps[:, MISC, 0:GB * (M + 1)], x2t[:, (g - 1) % 2, :],
                                 diag[:, (g - 1) % 2, :, :].rearrange("p b m -> p (b m)"),
                                 start=True, stop=True).then_inc(s_misc, 1)

            def layer3(bank, n, fields):
                for m in fields:
                    mm = nc.tensor.matmul(ps[:, bank, 0:n], k2w[:, m, :], gsb[:, m, 0:n],
                                          start=(m == 0), stop=(m == M - 1))
                return mm

            def tile(t, last):
                for k in range(TSLOTS):
                    q, s = divmod(k, SLOTS)
                    c = t * CHUNKS + q
                    g, n, b = k // BLOCKS, s // BLOCKS, k % BLOCKS
                    if s == 0:
                        pe.wait_ge(s_x1l, c + (BASE + 1))
                    old = k - BLK_BANKS
                    if share(old) == "Y":
                        pe.wait_ge(s_y4, t * (R * NY) + (BASE + R * count("Y", old)))
                    else:
                        pe.wait_ge(s_z4, t * NZ + (BASE + count("Z", old)))
                    cols = slice(n * P, (n + 1) * P)
                    for i, (x_, w_) in enumerate(((x1h, k1h), (x1h, k1l), (x1l, k1h))):
                        mm = nc.tensor.matmul(ps[:, k % BLK_BANKS, :], x_[:, q % 2, cols],
                                              w_[:, R * b:R * (b + 1), :].rearrange("p m o -> p (m o)"),
                                              start=(i == 0), stop=(i == 2))
                    mm.then_inc(s_blk, 1)
                    if not (last and q == CHUNKS - 1):
                        nq = (q + 1) % CHUNKS
                        for i in range(K1B):
                            if s == AT_V[i]:
                                if q == 0 and i == 0:
                                    pe.wait_ge(s_z3, t + BASE)
                                rotated(c + 1, nq, i)
                            if s == AT_V[i] + MM_LAG:
                                layer1(c + 1, nq, i)
                    if q == CHUNKS - 1 and AT_L3 <= s < AT_L3_END and not last:
                        if s == AT_L3:
                            pe.wait_ge(s_p1, (c + 1) * K1B + (BASE + K1B - 1))
                            pe.wait_ge(s_took, misc_count(t, q, "G", (AT_L3 - 1) // BLOCKS, last))
                        mm = layer3(L3_BANK, P, range((s - AT_L3) * L3_STEP, (s - AT_L3 + 1) * L3_STEP))
                        if s == AT_L3_END - 1:
                            mm.then_inc(s_l3, 1)
                    for at, what, i in misc_items(q, last):
                        if at != s:
                            continue
                        value = misc_count(t, q, what, i, last)
                        if what == "U1":
                            three_copies((q + 1) % CHUNKS, value)
                        if what == "PICK":
                            turn_back((q + 1) % CHUNKS, value)
                        if what == "T":
                            pe.wait_ge(s_parts, t + (BASE + 2))
                            bank_free(value)
                            turn(i, MISC, s_misc)
                        if what == "G":
                            contract(g, t * TG + (BASE + g + 1), t * TG + (BASE + g), value)

            pe.wait_ge(s_sel, 1)
            pe.wait_ge(s_part0, BASE)
            for i in range(WARM):
                nc.tensor.matmul(ps[0:KP, L3_BANK, :], rot[:, 0:KP], rot[:, 0:CH], start=True, stop=True)
            pe.wait_ge(s_parts, BASE + 1)
            for i in range(D // DT):
                turn(i, i, s_turned)
            pe.wait_ge(s_x0s, D // DT)
            three_copies(0, BASE + 1)
            rotated(0, 0, 0)
            turn_back(0, BASE + 2)
            rotated(0, 0, 1)
            pe.wait_ge(s_k0w, 1)
            for i in range(K1B):
                layer1(0, 0, i)
                if i + 2 < K1B:
                    rotated(0, 0, i + 2)
            pe.wait_ge(s_x0s, 2 * (D // DT))
            pe.wait_ge(s_k1l, 5)
            pe.wait_ge(s_zero, 5)
            pe.wait_ge(s_tail, 8 * 16)
            pe.wait_ge(s_took, BASE + MISC0)
            tile_loop(pe, tile)
            end = misc_count(TILES - 1, CHUNKS - 1, "G", NG - 1, True)
            pe.wait_ge(s_z1, BASE + TILES * CHUNKS)
            pe.wait_ge(s_z3, BASE + TILES - 1)

            def top1(i, k, start=False, stop=False):
                w, z = ((w1[:, 0, :], z1[:, :]), (w1[:, 1, :], z2[:, LAG:]), (w1[:, 2, :], z3[:, LAG:]),
                        (w1d[:, :], dense[:, :]))[k]
                return nc.tensor.matmul(ps[:, H1_BANKS[i], :], w[:, i * P:(i + 1) * P], z, start=start, stop=stop)

            for i in range(2):
                top1(i, 0, start=True)
                top1(i, 3)
            contract(TG, BASE + TILES * TG + 1, BASE + TILES * TG, end + 1)
            top1(2, 0, start=True)
            top1(2, 3)
            pe.wait_ge(s_took, end + 1)
            layer3(MISC, P + LAG, range(M)).then_inc(s_misc, 1)
            pe.wait_ge(s_y4, BASE + TILES * R * NY)
            pe.wait_ge(s_z4, BASE + TILES * NZ)
            top1(3, 0, start=True)
            top1(3, 3)
            pe.wait_ge(s_z2, BASE + TILES)
            for i in range(N1 // P):
                top1(i, 1)
            pe.wait_ge(s_z3, BASE + TILES)
            for i in range(N1 // P):
                top1(i, 2, stop=True).then_inc(s_h1_ps, 1)
            for i in range(N2 // P):
                for k in range(N1 // P):
                    pe.wait_ge(s_h1, k + 1)
                    mm = nc.tensor.matmul(ps[:, H2_BANKS[i], :], w2[:, k, i * P:(i + 1) * P], h1[:, k, :],
                                          start=(k == 0), stop=(k == N1 // P - 1))
                mm.then_inc(s_h2_ps, 1)
            for k in range(N2 // P):
                pe.wait_ge(s_h2, k + 1)
                mm = nc.tensor.matmul(ps[0:1, Y_BANK, :], w3[:, k:k + 1], h2[:, k, :],
                                      start=(k == 0), stop=(k == N2 // P - 1))
            mm.then_inc(s_y_ps, 1)


def lay_out(inputs):
    import numpy as np

    a = {f"tbl_{m}": inputs[f"tbl_{m}"] for m in range(M)}
    a["ids"] = inputs["ids"]
    a["dense"] = inputs["dense_ctx"].T
    k0 = inputs["L0_rec_k0"].transpose(1, 2, 0)
    straight = np.zeros((KP, K1B, H), k0.dtype)
    turned = np.zeros((KP, K1B, H), k0.dtype)
    fields = np.arange(M)
    for s in range(SHIFTS):
        k, i = divmod(s, S_IN)
        other = (fields + s) % M
        straight[i * M:(i + 1) * M, k] = k0[fields, other]
        if 0 < s < M // 2:
            turned[i * M:(i + 1) * M, k] = k0[other, fields]
    a["k0_straight"] = straight
    a["k0_turned"] = turned.reshape(KP, K1B * H)
    a["k1"] = inputs["L0_rec_k1"].transpose(1, 2, 0)
    a["k2"] = inputs["L0_rec_k2"].transpose(1, 2, 0)
    a["W_top1"] = inputs["W_top1"]
    a["W_top2"] = inputs["W_top2"]
    a["w3"] = inputs["W_top3"].reshape(N2 // P, P).T
    a["b1"] = inputs["b_top1"].reshape(N1 // P, P).T
    a["b2"] = inputs["b_top2"].reshape(N2 // P, P).T
    m_of = np.arange(XK) % M
    rows = np.arange(KP)
    shift = [(rows % M + k * S_IN + rows // M) % M for k in range(K1B)] + [rows % M]
    consts = np.zeros((P, (K1B + 1) * KP + M + P), np.float32)
    consts[0:XK, 0:(K1B + 1) * KP] = m_of[:, None] == np.concatenate(shift)[None, :]
    consts[0:XK, (K1B + 1) * KP:(K1B + 1) * KP + M] = m_of[:, None] == fields[None, :]
    consts[:, (K1B + 1) * KP + M:] = np.eye(P)
    a["consts"] = consts
    a["mask"] = (np.arange(P)[:, None] // D == np.arange(GB)[None, :]).astype(np.float32)
    return {k: np.ascontiguousarray(v) for k, v in a.items()}


def kernel(**inputs):
    import numpy as np
    import concourse.bacc as bacc
    from concourse.bass_utils import run_bass_kernel_spmd

    nc = bacc.Bacc("TRN2", target_bir_lowering=False, num_devices=1)
    laid = lay_out({k: np.asarray(v) for k, v in inputs.items()})
    tensors = {k: nc.dram_tensor(f"in_{k}", v.shape, mybir.dt.from_np(v.dtype), kind="ExternalInput").ap()
               for k, v in laid.items()}
    out = nc.dram_tensor("out_y", (B, 1), F32, kind="ExternalOutput").ap()
    tensors["out"] = out.rearrange("b o -> o b")
    build(nc, tensors)
    r = run_bass_kernel_spmd(nc, [{f"in_{k}": v for k, v in laid.items()}], core_ids=[0])
    return r.results[0]["out_y"]
```

```python
from contextlib import ExitStack

import concourse.bass as bass
from concourse import mybir

F32 = mybir.dt.float32
F32R = mybir.dt.float32r
BF16 = mybir.dt.bfloat16
I32 = mybir.dt.int32
ALU = mybir.AluOpType
ACT = mybir.ActivationFunctionType
AX = mybir.AxisListType

B = 512
M = 40
D = 16
H = 128
DENSE = 16
N1, N2 = 512, 256

P = 128
TILES = B // P
CH = 512
CHUNKS = D * P // CH
GB = P // D
NG = CH // P
TG = NG * CHUNKS
DT = 8
PARTS = 3
XK = PARTS * M

SHIFTS = M // 2 + 1
S_IN = P // M
KP = S_IN * M
K1B = SHIFTS // S_IN
COPIES = (K1B + 1) * KP
P1_RING = 4
V_RING = 4

R = 4
BLOCKS = M // R
SLOTS = NG * BLOCKS
TSLOTS = CHUNKS * SLOTS
SHARE = "YZYZYZYZYZ"
AHEAD = 10
GATHER_AT = [(CHUNKS - 1) * SLOTS + m * SLOTS // AHEAD for m in range(AHEAD)]
GATHER_AT += [(m - AHEAD) * 10 // 3 for m in range(AHEAD, M)]
BLK_BANKS = 4
TMP_RING = 4
ACC = 2

AT_U1, AT_PICK = 0, 11
AT_PAIRS = [5 + 4 * i for i in range(K1B)]
MM_LAG = 4
AT_X1 = 35
AT_G = 7
AT_FINAL, AT_DIAG = 3, 5
AT_TURN = (31, 34)
AT_SPLIT = 22
AT_L3 = 29
L3_STEP = 5
AT_L3_END = AT_L3 + M // L3_STEP

FIRST = 32
WARM = 30

LAG = 2 * GB

BASE = 64


def share(k):
    return SHARE[k % BLOCKS]


def count(kind, k):
    if k < 0:
        return count(kind, k + TSLOTS) - count(kind, TSLOTS - 1)
    return sum(share(x) == kind for x in range(k + 1))


def adds(k):
    if k < 0:
        return adds(k + TSLOTS) - adds(TSLOTS - 1)
    return sum(share(x) == "Z" and not first_of(x) for x in range(k + 1))


def first_of(k):
    return share(k) not in [share(x) for x in range(k // BLOCKS * BLOCKS, k)]


NY, NZ, NADD = count("Y", TSLOTS - 1), count("Z", TSLOTS - 1), adds(TSLOTS - 1)


def misc_items(q, last):
    items = [(AT_G + BLOCKS * n, "G", n) for n in range(NG)]
    if not (last and q == CHUNKS - 1):
        items += [(AT_U1, "U1", 0), (AT_PICK, "PICK", 0)]
    if q == CHUNKS - 2 and not last:
        items += [(at, "T", i) for i, at in enumerate(AT_TURN)]
    return sorted(items)


MISC0 = 2
NMISC = sum(len(misc_items(q, False)) for q in range(CHUNKS))

assert NADD % TMP_RING == 0 and TSLOTS % BLK_BANKS == 0 and CHUNKS * K1B % P1_RING == 0 and CHUNKS * K1B % V_RING == 0


def misc_of(q, what, i, last):
    before = sum(len(misc_items(x, last)) for x in range(q))
    return before + [x[1:] for x in misc_items(q, last)].index((what, i))


def build(nc, t_):
    ctx = ExitStack()
    with ctx:
        def sb(name, shape, dt=F32):
            return ctx.enter_context(nc.sbuf_tensor(name, shape, dt))

        ids_now = sb("ids_now", [P, M], I32)
        emb = sb("emb", [P, M * D])
        rest = sb("rest", [P, D, M])
        parts = sb("parts", [P, D, XK], BF16)
        x0s = sb("x0s", [XK, CHUNKS * CH], BF16)
        x0t = sb("x0t", [P, 2, NG, M])
        u1 = sb("u1", [KP, CH])
        v = sb("v", [KP, V_RING, CH])
        p1 = sb("p1", [KP, P1_RING, CH])
        x1h = sb("x1h", [H, 2, CH], F32R)
        x1l = sb("x1l", [H, 2, CH], F32R)
        acc = sb("acc", [P, 2, ACC + R, H])
        tmp_z = sb("tmp_z", [P, TMP_RING, R, H])
        x2t = sb("x2t", [P, 2, H])
        diag = sb("diag", [P, 2, GB, M + 1])
        mask = sb("mask", [P, GB])
        gsb = sb("gsb", [H, M + 1, P + LAG])
        k1h = sb("k1h", [H, M, H], F32R)
        k1l = sb("k1l", [H, M, H], F32R)
        k1raw = sb("k1raw", [H, M, H])
        k2w = sb("k2w", [H, M, H])
        k0w = sb("k0w", [KP, K1B, H])
        k0_turned = sb("k0_turned", [KP, K1B * H])
        copies = sb("copies", [XK, COPIES], BF16)
        pick = sb("pick", [XK, M], BF16)
        ident_b = sb("ident_b", [P, P], BF16)
        consts = sb("consts", [P, COPIES + M + P])
        z1 = sb("z1", [P, B])
        z2 = sb("z2", [P, LAG + B])
        z3 = sb("z3", [P, LAG + B])
        dense = sb("dense", [DENSE, B])
        w1 = sb("w1", [P, 3, N1])
        w1d = sb("w1d", [DENSE, N1])
        w2 = sb("w2", [P, N1 // P, N2])
        w3 = sb("w3", [P, N2 // P])
        b1 = sb("b1", [P, N1 // P])
        b2 = sb("b2", [P, N2 // P])
        top = k1raw[:, :, :].rearrange("p m o -> p (m o)")
        h1 = top[:, 0:N1 // P * B].rearrange("p (i b) -> p i b", b=B)
        h2 = top[:, N1 // P * B:(N1 + N2) // P * B].rearrange("p (i b) -> p i b", b=B)
        y = sb("y", [1, B])

        ps = ctx.enter_context(nc.psum_tensor("ps", [P, 8, CH], F32))
        ACC1, L3_BANK, MISC = 4, 5, 7
        V_BANKS = (5, 6)
        H1_BANKS, H2_BANKS, Y_BANK = (4, 5, 6, 0), (1, 2), 3

        def sem(name):
            return ctx.enter_context(nc.semaphore(name))

        s_ids = sem("s_ids")
        s_const = sem("s_const")
        s_k0 = sem("s_k0")
        s_k1 = sem("s_k1")
        s_mask = sem("s_mask")
        s_tail = sem("s_tail")
        s_first = sem("s_first")
        s_gather = sem("s_gather")
        s_v = [sem(f"s_v{i}") for i in range(V_RING)]
        s_out = sem("s_out")
        s_sel = sem("s_sel")
        s_k1h = sem("s_k1h")
        s_k1l = sem("s_k1l")
        s_k0w = sem("s_k0w")
        s_zero = sem("s_zero")
        s_v_first = sem("s_v_first")
        s_turned = sem("s_turned")
        s_x0s = sem("s_x0s")
        s_h1_ps, s_h1, s_h2_ps, s_h2, s_y_ps, s_y = (sem(x) for x in ("s_h1_ps", "s_h1", "s_h2_ps", "s_h2", "s_y_ps", "s_y"))
        s_part0 = sem("s_part0")
        s_rest = sem("s_rest")
        s_part1 = sem("s_part1")
        s_parts = sem("s_parts")
        s_misc = sem("s_misc")
        s_took = sem("s_took")
        s_p1 = sem("s_p1")
        s_mm1 = sem("s_mm1")
        s_x1h = sem("s_x1h")
        s_x1l = sem("s_x1l")
        s_z1 = sem("s_z1")
        s_blk = sem("s_blk")
        s_y4 = sem("s_y4")
        s_z4 = sem("s_z4")
        s_add = sem("s_add")
        s_x2t = sem("s_x2t")
        s_diag = sem("s_diag")
        s_l3 = sem("s_l3")
        s_z3 = sem("s_z3")
        s_z2 = sem("s_z2")
        passed = sem("passed")

        def wait_alone(eng, s, value):
            eng.wait_ge(s, value)
            eng.sem_inc(passed, 1)

        def misc_count(t, q, what, i, last):
            return t * NMISC + (BASE + MISC0 + misc_of(q, what, i, last) + 1)

        def gathered(t):
            return t * (M * 16) + (M - FIRST) * 16

        def split_range(part):
            return (slice(0, FIRST), slice(FIRST, M), slice(0, M))[part]

        def tile_loop(eng, body):
            with eng.Fori(0, TILES - 1) as t:
                body(t, False)
            body(TILES - 1, True)

        block = ctx.enter_context(nc.Block())

        @block.sync
        def _(sp):
            def load(out, name, s):
                sp.dma_start(out, t_[name]).then_inc(s, 16)

            sp.dma_start(ids_now[:, :], t_["ids"][0:P, :]).then_inc(s_ids, 16)
            for at in range(K1B):
                sp.sem_inc(s_v[at % V_RING], S_IN * 16)
            load(consts[:, :], "consts", s_const)
            load(k0w[:, :, :], "k0_straight", s_k0)
            load(k0_turned[:, :], "k0_turned", s_k0)
            load(mask[:, :], "mask", s_mask)
            load(k1raw[:, :, :], "k1", s_k1)
            load(k2w[:, :, :], "k2", s_tail)
            sp.dma_start(w1[:, :, :], t_["W_top1"][0:3 * P, :].rearrange("(k p) n -> p k n", p=P)
                         ).then_inc(s_tail, 16)
            sp.dma_start(w1d[:, :], t_["W_top1"][3 * P:3 * P + DENSE, :]).then_inc(s_tail, 16)
            sp.dma_start(w2[:, :, :], t_["W_top2"].rearrange("(k p) n -> p k n", p=P)).then_inc(s_tail, 16)
            load(w3[:, :], "w3", s_tail)
            load(b1[:, :], "b1", s_tail)
            load(b2[:, :], "b2", s_tail)
            load(dense[:, :], "dense", s_tail)

            def shift(c, q, value):
                wait_alone(sp, s_took, value)
                for i in range(K1B):
                    wait_alone(sp, s_p1, c * K1B + (BASE + i + 1 - V_RING))
                    slot = (K1B * q + i) % V_RING
                    for j in range(S_IN):
                        s = S_IN * i + j
                        sp.dma_start(v[j * M:(j + 1) * M, slot, :], u1[s:s + M, :]).then_inc(s_v[slot], 16)

            def load_ids(rows, t):
                wait_alone(sp, s_gather, gathered(t))
                sp.dma_start(ids_now[:, :], t_["ids"][rows, :]).then_inc(s_ids, 16)

            def tile(t, last):
                for q in range(CHUNKS):
                    if not (last and q == CHUNKS - 1):
                        shift(t * CHUNKS + (q + 1), (q + 1) % CHUNKS, misc_count(t, q, "U1", 0, last))
                    if q == CHUNKS - 2 and not last:
                        load_ids(bass.ds(t * P + 2 * P, P), t + 1)

            sp.wait_ge(s_first, FIRST * 16)
            load_ids(slice(P, 2 * P), 0)
            tile_loop(sp, tile)
            sp.wait_ge(s_y, 1)
            sp.dma_start(t_["out"], y[:, :]).then_inc(s_out, 16)
            sp.wait_ge(s_out, 16)

        @block.gpsimd
        def _(pool):
            pool.sem_inc(s_add, BASE)

            def gather(m, s):
                nc.gpsimd.indirect_dma_start(
                    emb[:, m * D:(m + 1) * D], None, t_[f"tbl_{m}"],
                    bass.IndirectOffsetOnAxis(ap=ids_now[:, m:m + 1], axis=0)).then_inc(s, 16)

            def tile(t, last):
                for k in range(TSLOTS):
                    if share(k) == "Z" and not first_of(k):
                        n = k // BLOCKS
                        wait_alone(pool, s_z4, t * NZ + (BASE + count("Z", k)))
                        wait_alone(pool, s_add, t * NADD + (BASE + adds(k) - 1))
                        nc.gpsimd.tensor_tensor(acc[:, n % 2, ACC:, :], acc[:, n % 2, ACC:, :],
                                                tmp_z[:, (adds(k) - 1) % TMP_RING, :, :],
                                                ALU.add).then_inc(s_add, 1)
                    if not last and k in GATHER_AT:
                        if k == GATHER_AT[0]:
                            ahead(t + 1)
                        gather(GATHER_AT.index(k), s_gather)

            def ahead(t):
                wait_alone(pool, s_ids, (t + 2) * 16)
                wait_alone(pool, s_rest, t + (BASE + 1))

            pool.wait_ge(s_ids, 16)
            for m in range(M):
                gather(m, s_first if m < FIRST else s_gather)
            ahead(0)
            for m in range(AHEAD):
                gather(m, s_gather)
            tile_loop(pool, tile)

        @block.scalar
        def _(act):
            for s in (s_took, s_x1h, s_z4, s_z2, s_z3):
                act.sem_inc(s, BASE)
            for s in (s_part0, s_part1):
                act.sem_inc(s, BASE - 1)
            act.wait_ge(s_const, 16)
            nc.scalar.copy(copies[:, :], consts[0:XK, 0:COPIES])
            nc.scalar.copy(pick[:, :], consts[0:XK, COPIES:COPIES + M])
            nc.scalar.copy(ident_b[:, :], consts[:, COPIES + M:COPIES + M + P]).then_inc(s_sel, 1)
            act.wait_ge(s_k1, 16)
            for i in range(5):
                m = slice(i * M // 5, (i + 1) * M // 5)
                nc.scalar.copy(k1h[:, m, :], k1raw[:, m, :]).then_inc(s_k1h, 1)

            emb_dm = emb[:, :].rearrange("p (m d) -> p d m", m=M)
            x0_db = x0s[:, :].rearrange("p (b d) -> p d b", d=D)

            def split0(t, part=2):
                act.wait_ge(s_gather, gathered(t)) if part else act.wait_ge(s_first, FIRST * 16)
                m = split_range(part)
                nc.scalar.copy(parts[:, :, m], emb_dm[:, :, m]).then_inc(s_part0, 1)

            def split1(t, part=2):
                act.wait_ge(s_rest, t + (BASE + min(part, 1)))
                m = split_range(part)
                nc.scalar.copy(parts[:, :, M + m.start:M + m.stop], rest[:, :, m]).then_inc(s_part1, 1)

            def took_turned(i, bank, b, s):
                nc.scalar.copy(x0_db[:, i * DT:(i + 1) * DT, b],
                               ps[0:XK, bank, :].bitcast(BF16)[:, 0:DT * P].rearrange("p (d b) -> p d b", d=DT)[:, :, b]
                               ).then_inc(s, 1)

            def took_u1(c, value):
                wait_alone(act, s_p1, c * K1B + BASE)
                act.wait_ge(s_misc, value)
                nc.scalar.copy(u1[:, :], ps[0:KP, MISC, :]).then_inc(s_took, 1)

            def took_pick(slot, diag_value, value):
                wait_alone(act, s_diag, diag_value)
                act.wait_ge(s_misc, value)
                nc.scalar.copy(x0t[:, slot, :, :],
                               ps[:, MISC, 0:NG * M].rearrange("p (n m) -> p n m", m=M)).then_inc(s_took, 1)

            def contracted(place):
                nc.scalar.copy(gsb[:, :, place * GB:(place + 1) * GB].rearrange("p m b -> p b m"),
                               ps[:, MISC, 0:GB * (M + 1)].rearrange("p (b m) -> p b m", b=GB)).then_inc(s_took, 1)

            def lead_x1(c, slot):
                wait_alone(act, s_blk, (c - 1) * SLOTS + BASE)
                act.wait_ge(s_mm1, (c + 1) * K1B + BASE)
                nc.scalar.copy(x1h[:, slot, :], ps[:, ACC1, :]).then_inc(s_x1h, 1)

            def tile(t, last):
                for k in range(TSLOTS):
                    q, s = divmod(k, SLOTS)
                    c = t * CHUNKS + q
                    g, n, b = k // BLOCKS, s // BLOCKS, k % BLOCKS
                    if share(k) == "Z":
                        wait_alone(act, s_blk, t * TSLOTS + (BASE + k + 1))
                        if first_of(k):
                            wait_alone(act, s_x2t, t * TG + (BASE + g))
                            out = acc[:, g % 2, ACC:, :]
                        else:
                            wait_alone(act, s_add, t * NADD + (BASE + adds(k) - TMP_RING))
                            out = tmp_z[:, (adds(k) - 1) % TMP_RING, :, :]
                        for r in range(R):
                            m = R * b + r
                            last_ = nc.scalar.activation(out[:, r, :], ps[:, k % BLK_BANKS, r * H:(r + 1) * H],
                                                         ACT.Copy, scale=x0t[:, q % 2, n, m:m + 1])
                        last_.then_inc(s_z4, 1)
                    if q == CHUNKS - 2 and not last:
                        if s == AT_SPLIT:
                            split0(t + 1)
                        if s == AT_SPLIT + 4:
                            split1(t + 1)
                    if q == CHUNKS - 1 and s == AT_L3_END and not last:
                        act.wait_ge(s_l3, t + (BASE + 1))
                        nc.scalar.copy(z3[:, bass.ds(t * P, P)], ps[:, L3_BANK, 0:P]).then_inc(s_z3, 1)
                        nc.scalar.copy(z2[:, bass.ds(t * P, P)], gsb[:, M, 0:P]).then_inc(s_z2, 1)
                    if s == AT_X1 and not (last and q == CHUNKS - 1):
                        lead_x1(c + 1, (q + 1) % 2)
                    for at, what, i in misc_items(q, last):
                        if at != s:
                            continue
                        value = misc_count(t, q, what, i, last)
                        if what == "U1":
                            took_u1(c + 1, value)
                        if what == "PICK":
                            took_pick((q + 1) % 2, c * NG + BASE, value)
                        if what == "T":
                            act.wait_ge(s_misc, value)
                            took_turned(i, MISC, slice(0, P), s_took)
                        if what == "G":
                            wait_alone(act, s_z2, t + (BASE + (g == TG - 1 and not last)))
                            wait_alone(act, s_misc, value)
                            place = g + 1 if last else (g + 1) % TG
                            contracted(place)

            split0(0, 0)
            split1(0, 0)
            split0(0, 1)
            split1(0, 1)
            for i in range(D // DT):
                act.wait_ge(s_turned, i + 1)
                took_turned(i, i, slice(0, CH // D), s_x0s)
            took_u1(0, BASE + 1)
            took_pick(0, BASE, BASE + 2)
            for i in range(D // DT):
                took_turned(i, i, slice(CH // D, P), s_x0s)
            lead_x1(0, 0)
            tile_loop(act, tile)

            end = misc_count(TILES - 1, CHUNKS - 1, "G", NG - 1, True)
            act.wait_ge(s_misc, end + 1)
            contracted(TG + 1)
            act.wait_ge(s_took, end + 1)
            nc.scalar.copy(z2[:, (TILES - 1) * P:], gsb[:, M, :]).then_inc(s_z2, 1)
            act.wait_ge(s_misc, end + 2)
            nc.scalar.copy(z3[:, (TILES - 1) * P:], ps[:, MISC, 0:P + LAG]).then_inc(s_z3, 1)
            act.wait_ge(s_tail, 8 * 16)
            for i in range(N1 // P):
                act.wait_ge(s_h1_ps, i + 1)
                nc.scalar.activation(h1[:, i, :], ps[:, H1_BANKS[i], :], ACT.Relu, bias=b1[:, i:i + 1]).then_inc(s_h1, 1)
            for i in range(N2 // P):
                act.wait_ge(s_h2_ps, i + 1)
                nc.scalar.activation(h2[:, i, :], ps[:, H2_BANKS[i], :], ACT.Relu, bias=b2[:, i:i + 1]).then_inc(s_h2, 1)
            act.wait_ge(s_y_ps, 1)
            nc.scalar.copy(y[:, :], ps[0:1, Y_BANK, :]).then_inc(s_y, 1)

        @block.vector
        def _(dve):
            for s in (s_p1, s_x1l, s_z1, s_y4, s_x2t, s_diag):
                dve.sem_inc(s, BASE)
            for s in (s_rest, s_parts):
                dve.sem_inc(s, BASE - 1)
            for buf in (acc[:, 1, :, :], diag[:, 1, :, 0:M], gsb[:, :, 0:GB]):
                nc.vector.memset(buf, 0.0).then_inc(s_zero, 1)
            dve.wait_ge(s_mask, 16)
            for i in range(2):
                nc.vector.tensor_copy(diag[:, i, :, M], mask[:, :]).then_inc(s_zero, 1)
            dve.wait_ge(s_zero, 5)
            dve.wait_ge(s_k0, 32)
            k0_flat = k0w[:, :, :].rearrange("p k o -> p (k o)")
            nc.vector.tensor_tensor(k0_flat, k0_flat, k0_turned[:, :], ALU.add).then_inc(s_k0w, 1)
            for i in range(5):
                m = slice(i * M // 5, (i + 1) * M // 5)
                dve.wait_ge(s_k1h, i + 1)
                nc.vector.tensor_tensor(k1l[:, m, :], k1raw[:, m, :], k1h[:, m, :].bitcast(F32),
                                        ALU.subtract).then_inc(s_k1l, 1)

            emb_dm = emb[:, :].rearrange("p (m d) -> p d m", m=M)

            def split_rest(t, part=2):
                dve.wait_ge(s_part0, t + (BASE + min(part, 1)))
                m = split_range(part)
                nc.vector.tensor_tensor(rest[:, :, m], emb_dm[:, :, m], parts[:, :, m], ALU.subtract).then_inc(s_rest, 1)

            def split2(t, part=2):
                dve.wait_ge(s_part1, t + (BASE + min(part, 1)))
                m = split_range(part)
                nc.vector.tensor_tensor(parts[:, :, 2 * M + m.start:2 * M + m.stop], rest[:, :, m],
                                        parts[:, :, M + m.start:M + m.stop], ALU.subtract).then_inc(s_parts, 1)

            def multiply(at, shifted):
                nc.vector.tensor_tensor(p1[:, at % P1_RING, :], u1[:, :], shifted, ALU.mult).then_inc(s_p1, 1)

            def pairs(t, q, i, u1_value):
                c, at = t * CHUNKS + q, K1B * q + i
                wait_alone(dve, s_v[at % V_RING],
                           t * (CHUNKS * K1B // V_RING * S_IN * 16) + (at // V_RING + 1) * (S_IN * 16))
                wait_alone(dve, s_mm1, c * K1B + (BASE + i + 1 - P1_RING))
                if i == 0:
                    wait_alone(dve, s_took, u1_value)
                multiply(at, v[:, at % V_RING, :])

            def rest_x1(c, slot, cols):
                wait_alone(dve, s_x1h, c + (BASE + 1))
                nc.vector.tensor_tensor(x1l[:, slot, :], ps[:, ACC1, :], x1h[:, slot, :].bitcast(F32),
                                        ALU.subtract).then_inc(s_x1l, 1)
                nc.vector.tensor_reduce(z1[:, cols], ps[:, ACC1, :].rearrange("p (b d) -> p b d", d=D),
                                        AX.X, ALU.add).then_inc(s_z1, 1)

            def final(t, g, contracted):
                slot = (g - 1) % 2
                k = g * BLOCKS - 1
                wait_alone(dve, s_y4, t * (R * NY) + (BASE + R * count("Y", k)))
                wait_alone(dve, s_add, t * NADD + (BASE + adds(k)))
                wait_alone(dve, s_misc, contracted)
                nc.vector.tensor_reduce(x2t[:, slot, :], acc[:, slot, :, :].rearrange("p r h -> p h r"),
                                        AX.X, ALU.add).then_inc(s_x2t, 1)

            def tile(t, last):
                for k in range(TSLOTS):
                    q, s = divmod(k, SLOTS)
                    c = t * CHUNKS + q
                    g, n, b = k // BLOCKS, s // BLOCKS, k % BLOCKS

                    def contracted(x):
                        if x >= 0:
                            return misc_count(t, (x + 1) // NG, "G", (x + 1) % NG, last)
                        return misc_count(t - 1, (x + 1 + TG) // NG, "G", (x + 1 + TG) % NG, False)

                    if share(k) == "Y":
                        wait_alone(dve, s_blk, t * TSLOTS + (BASE + k + 1))
                        done = BASE + R * (count("Y", k) - 1)
                        if first_of(k):
                            wait_alone(dve, s_x2t, t * TG + (BASE + g))
                        for r in range(R):
                            m = R * b + r
                            out = acc[:, g % 2, r % ACC, :]
                            src = ps[:, k % BLK_BANKS, r * H:(r + 1) * H]
                            factor = x0t[:, q % 2, n, m:m + 1]
                            if first_of(k) and r < ACC:
                                nc.vector.tensor_scalar(out, src, factor, None, ALU.mult).then_inc(s_y4, 1)
                            else:
                                wait_alone(dve, s_y4, t * (R * NY) + (done + r - ACC + 1))
                                nc.vector.scalar_tensor_tensor(out=out, in0=src, scalar=factor, in1=out,
                                                               op0=ALU.mult, op1=ALU.add).then_inc(s_y4, 1)
                    if b == AT_FINAL:
                        final(t, g, contracted(g - 3))
                    if b == AT_DIAG:
                        wait_alone(dve, s_misc, contracted(g - 2))
                        wait_alone(dve, s_blk, t * TSLOTS + (BASE + q * SLOTS + 1))
                        nc.vector.tensor_tensor(diag[:, g % 2, :, 0:M],
                                                x0t[:, q % 2, n, :].unsqueeze(1).to_broadcast([P, GB, M]),
                                                mask[:, :].unsqueeze(2).to_broadcast([P, GB, M]),
                                                ALU.mult).then_inc(s_diag, 1)
                    if not (last and q == CHUNKS - 1):
                        for i in range(K1B):
                            if s == AT_PAIRS[i]:
                                pairs(t + (q + 1) // CHUNKS, (q + 1) % CHUNKS, i, misc_count(t, q, "U1", 0, last))
                        if s == AT_X1 + 1:
                            rest_x1(c + 1, (q + 1) % 2, bass.ds((c + 1) * (CH // D), CH // D) if not last
                                    else slice((c + 1) * (CH // D), (c + 2) * (CH // D)))
                    if q == CHUNKS - 2 and not last:
                        if s == AT_SPLIT + 2:
                            split_rest(t + 1)
                        if s == AT_SPLIT + 6:
                            split2(t + 1)

            for part in range(2):
                split_rest(0, part)
                split2(0, part)
            for i in range(K1B):
                dve.wait_ge(s_v_first, i + 1)
                if i >= P1_RING:
                    dve.wait_ge(s_mm1, BASE + i + 1 - P1_RING)
                if i == 0:
                    dve.wait_ge(s_took, BASE + 1)
                multiply(i, ps[0:KP, V_BANKS[i % 2], :])
            rest_x1(0, 0, slice(0, CH // D))
            tile_loop(dve, tile)
            final(TILES - 1, TG, misc_count(TILES - 1, (TG - 2) // NG, "G", (TG - 2) % NG, True))

        @block.tensor
        def _(pe):
            for s in (s_misc, s_mm1, s_blk, s_l3):
                pe.sem_inc(s, BASE)

            def bank_free(value):
                pe.wait_ge(s_took, value - 1)

            def turn(i, bank, s):
                out = ps[0:XK, bank, :].bitcast(BF16)
                for d in range(DT):
                    last = nc.tensor.transpose(out[:, d * P:(d + 1) * P], parts[:, i * DT + d, :], ident_b[:, :])
                last.then_inc(s, 1)

            def three_copies(q, value):
                bank_free(value)
                nc.tensor.matmul(ps[0:KP, MISC, :], copies[:, 0:KP], x0s[:, q * CH:(q + 1) * CH],
                                 start=True, stop=True).then_inc(s_misc, 1)

            def turn_back(q, value):
                bank_free(value)
                for n in range(NG):
                    col = q * CH + n * P
                    last = nc.tensor.matmul(ps[:, MISC, n * M:(n + 1) * M], x0s[:, col:col + P], pick[:, :],
                                            start=True, stop=True)
                last.then_inc(s_misc, 1)

            def shifted(i):
                if i >= 2:
                    pe.wait_ge(s_p1, BASE + i - 1)
                nc.tensor.matmul(ps[0:KP, V_BANKS[i % 2], :], copies[:, (i + 1) * KP:(i + 2) * KP], x0s[:, 0:CH],
                                 start=True, stop=True).then_inc(s_v_first, 1)

            def layer1(c, q, i):
                if i == 0:
                    pe.wait_ge(s_z1, c + BASE)
                pe.wait_ge(s_p1, c * K1B + (BASE + i + 1))
                nc.tensor.matmul(ps[:, ACC1, :], k0w[:, i, :], p1[:, (K1B * q + i) % P1_RING, :],
                                 start=(i == 0), stop=(i == K1B - 1)).then_inc(s_mm1, 1)

            def contract(g, x2t_value, diag_value, value):
                pe.wait_ge(s_x2t, x2t_value)
                pe.wait_ge(s_diag, diag_value)
                bank_free(value)
                nc.tensor.matmul(ps[:, MISC, 0:GB * (M + 1)], x2t[:, (g - 1) % 2, :],
                                 diag[:, (g - 1) % 2, :, :].rearrange("p b m -> p (b m)"),
                                 start=True, stop=True).then_inc(s_misc, 1)

            def layer3(bank, n, fields):
                for m in fields:
                    mm = nc.tensor.matmul(ps[:, bank, 0:n], k2w[:, m, :], gsb[:, m, 0:n],
                                          start=(m == 0), stop=(m == M - 1))
                return mm

            def tile(t, last):
                for k in range(TSLOTS):
                    q, s = divmod(k, SLOTS)
                    c = t * CHUNKS + q
                    g, n, b = k // BLOCKS, s // BLOCKS, k % BLOCKS
                    if s == 0:
                        pe.wait_ge(s_x1l, c + (BASE + 1))
                    old = k - BLK_BANKS
                    if share(old) == "Y":
                        pe.wait_ge(s_y4, t * (R * NY) + (BASE + R * count("Y", old)))
                    else:
                        pe.wait_ge(s_z4, t * NZ + (BASE + count("Z", old)))
                    cols = slice(n * P, (n + 1) * P)
                    for i, (x_, w_) in enumerate(((x1h, k1h), (x1h, k1l), (x1l, k1h))):
                        mm = nc.tensor.matmul(ps[:, k % BLK_BANKS, :], x_[:, q % 2, cols],
                                              w_[:, R * b:R * (b + 1), :].rearrange("p m o -> p (m o)"),
                                              start=(i == 0), stop=(i == 2))
                    mm.then_inc(s_blk, 1)
                    if not (last and q == CHUNKS - 1):
                        nq = (q + 1) % CHUNKS
                        for i in range(K1B):
                            if s == AT_PAIRS[i] + MM_LAG:
                                layer1(c + 1, nq, i)
                    if q == CHUNKS - 1 and AT_L3 <= s < AT_L3_END and not last:
                        if s == AT_L3:
                            pe.wait_ge(s_z3, t + BASE)
                            pe.wait_ge(s_took, misc_count(t, q, "G", (AT_L3 - 1) // BLOCKS, last))
                        mm = layer3(L3_BANK, P, range((s - AT_L3) * L3_STEP, (s - AT_L3 + 1) * L3_STEP))
                        if s == AT_L3_END - 1:
                            mm.then_inc(s_l3, 1)
                    for at, what, i in misc_items(q, last):
                        if at != s:
                            continue
                        value = misc_count(t, q, what, i, last)
                        if what == "U1":
                            three_copies((q + 1) % CHUNKS, value)
                        if what == "PICK":
                            turn_back((q + 1) % CHUNKS, value)
                        if what == "T":
                            pe.wait_ge(s_parts, t + (BASE + 2))
                            bank_free(value)
                            turn(i, MISC, s_misc)
                        if what == "G":
                            contract(g, t * TG + (BASE + g + 1), t * TG + (BASE + g), value)

            pe.wait_ge(s_k1h, 1)
            pe.wait_ge(s_part0, BASE)
            for i in range(WARM):
                nc.tensor.matmul(ps[:, L3_BANK, :], k1h[:, 0, :], k1h[:, 0:R, :].rearrange("p m o -> p (m o)"),
                                 start=True, stop=True)
            pe.wait_ge(s_sel, 1)
            pe.wait_ge(s_parts, BASE + 1)
            for i in range(D // DT):
                turn(i, i, s_turned)
            pe.wait_ge(s_x0s, D // DT)
            three_copies(0, BASE + 1)
            shifted(0)
            turn_back(0, BASE + 2)
            shifted(1)
            pe.wait_ge(s_k0w, 1)
            for i in range(K1B):
                layer1(0, 0, i)
                if i + 2 < K1B:
                    shifted(i + 2)
            pe.wait_ge(s_x0s, 2 * (D // DT))
            pe.wait_ge(s_k1l, 5)
            pe.wait_ge(s_zero, 5)
            pe.wait_ge(s_tail, 8 * 16)
            pe.wait_ge(s_took, BASE + MISC0)
            tile_loop(pe, tile)
            end = misc_count(TILES - 1, CHUNKS - 1, "G", NG - 1, True)
            pe.wait_ge(s_z1, BASE + TILES * CHUNKS)
            pe.wait_ge(s_z3, BASE + TILES - 1)

            def top1(i, k, start=False, stop=False):
                w, z = ((w1[:, 0, :], z1[:, :]), (w1[:, 1, :], z2[:, LAG:]), (w1[:, 2, :], z3[:, LAG:]),
                        (w1d[:, :], dense[:, :]))[k]
                return nc.tensor.matmul(ps[:, H1_BANKS[i], :], w[:, i * P:(i + 1) * P], z, start=start, stop=stop)

            for i in range(2):
                top1(i, 0, start=True)
                top1(i, 3)
            contract(TG, BASE + TILES * TG + 1, BASE + TILES * TG, end + 1)
            top1(2, 0, start=True)
            top1(2, 3)
            pe.wait_ge(s_took, end + 1)
            layer3(MISC, P + LAG, range(M)).then_inc(s_misc, 1)
            pe.wait_ge(s_y4, BASE + TILES * R * NY)
            pe.wait_ge(s_z4, BASE + TILES * NZ)
            top1(3, 0, start=True)
            top1(3, 3)
            pe.wait_ge(s_z2, BASE + TILES)
            for i in range(N1 // P):
                top1(i, 1)
            pe.wait_ge(s_z3, BASE + TILES)
            for i in range(N1 // P):
                top1(i, 2, stop=True).then_inc(s_h1_ps, 1)
            for i in range(N2 // P):
                for k in range(N1 // P):
                    pe.wait_ge(s_h1, k + 1)
                    mm = nc.tensor.matmul(ps[:, H2_BANKS[i], :], w2[:, k, i * P:(i + 1) * P], h1[:, k, :],
                                          start=(k == 0), stop=(k == N1 // P - 1))
                mm.then_inc(s_h2_ps, 1)
            for k in range(N2 // P):
                pe.wait_ge(s_h2, k + 1)
                mm = nc.tensor.matmul(ps[0:1, Y_BANK, :], w3[:, k:k + 1], h2[:, k, :],
                                      start=(k == 0), stop=(k == N2 // P - 1))
            mm.then_inc(s_y_ps, 1)


def lay_out(inputs):
    import numpy as np

    a = {f"tbl_{m}": inputs[f"tbl_{m}"] for m in range(M)}
    a["ids"] = np.concatenate([inputs["ids"], inputs["ids"][B - P:]])
    a["dense"] = inputs["dense_ctx"].T
    k0 = inputs["L0_rec_k0"].transpose(1, 2, 0)
    straight = np.zeros((KP, K1B, H), k0.dtype)
    turned = np.zeros((KP, K1B, H), k0.dtype)
    fields = np.arange(M)
    for s in range(SHIFTS):
        k, i = divmod(s, S_IN)
        other = (fields + s) % M
        straight[i * M:(i + 1) * M, k] = k0[fields, other]
        if 0 < s < M // 2:
            turned[i * M:(i + 1) * M, k] = k0[other, fields]
    a["k0_straight"] = straight
    a["k0_turned"] = turned.reshape(KP, K1B * H)
    a["k1"] = inputs["L0_rec_k1"].transpose(1, 2, 0)
    a["k2"] = inputs["L0_rec_k2"].transpose(1, 2, 0)
    a["W_top1"] = inputs["W_top1"]
    a["W_top2"] = inputs["W_top2"]
    a["w3"] = inputs["W_top3"].reshape(N2 // P, P).T
    a["b1"] = inputs["b_top1"].reshape(N1 // P, P).T
    a["b2"] = inputs["b_top2"].reshape(N2 // P, P).T
    m_of = np.arange(XK) % M
    rows = np.arange(KP)
    field = [rows % M] + [(rows % M + k * S_IN + rows // M) % M for k in range(K1B)]
    consts = np.zeros((P, COPIES + M + P), np.float32)
    consts[0:XK, 0:COPIES] = m_of[:, None] == np.concatenate(field)[None, :]
    consts[0:XK, COPIES:COPIES + M] = m_of[:, None] == fields[None, :]
    consts[:, COPIES + M:] = np.eye(P)
    a["consts"] = consts
    a["mask"] = (np.arange(P)[:, None] // D == np.arange(GB)[None, :]).astype(np.float32)
    return {k: np.ascontiguousarray(v) for k, v in a.items()}


def kernel(**inputs):
    import numpy as np
    import concourse.bacc as bacc
    from concourse.bass_utils import run_bass_kernel_spmd

    nc = bacc.Bacc("TRN2", target_bir_lowering=False, num_devices=1)
    laid = lay_out({k: np.asarray(v) for k, v in inputs.items()})
    tensors = {k: nc.dram_tensor(f"in_{k}", v.shape, mybir.dt.from_np(v.dtype), kind="ExternalInput").ap()
               for k, v in laid.items()}
    out = nc.dram_tensor("out_y", (B, 1), F32, kind="ExternalOutput").ap()
    tensors["out"] = out.rearrange("b o -> o b")
    build(nc, tensors)
    r = run_bass_kernel_spmd(nc, [{f"in_{k}": v for k, v in laid.items()}], core_ids=[0])
    return r.results[0]["out_y"]
```
